# Optimizing a Trainium2 kernel written in Bass

```python
import numpy as np
import jax
import jax.numpy as jnp

def _softmax(x, axis=-1):
    return jax.nn.softmax(x, axis=axis)

def _gelu(x):
    return jax.nn.gelu(x, approximate=True)

def _silu(x):
    return jax.nn.silu(x)

def _sigmoid(x):
    return jax.nn.sigmoid(x)

def _layernorm(x, axis=-1, eps=1e-05):
    m = jnp.mean(x, axis=axis, keepdims=True)
    v = jnp.var(x, axis=axis, keepdims=True)
    return (x - m) / jnp.sqrt(v + eps)

def _scatter_add(tgt, idx, src, axis=0):
    return tgt.at[idx].add(src)

def _segment_sum(src, seg, n):
    return jax.ops.segment_sum(src, seg, n)
kernel_name = 'mk_recurrent_d1_jaxref_r8_622ddb'

def setup_inputs(seed: int=0):
    np.random.seed(seed)
    _w = jnp.asarray

    def _L0_attn_setup():
        import jax, jax.numpy as jnp
        import numpy as np
        import math
        B, S, DM = (1, 256, 512)
        H, HKV, HD = (32, 8, 128)
        EPS = 1e-06
        NEG_INF = -1e+30

        def _alibi_slopes(n_heads: int) -> np.ndarray:
            start = 2 ** (-2 ** (-(math.log2(n_heads) - 3)))
            return np.array([start * start ** i for i in range(n_heads)], dtype=np.float32)

        def _rmsnorm(t, w):
            tf = t.astype(jnp.float32)
            inv = jax.lax.rsqrt(jnp.mean(tf * tf, axis=-1, keepdims=True) + EPS)
            return (tf * inv * w).astype(t.dtype)
        key = jax.random.key(seed)
        ks = jax.random.split(key, 5)
        std = 0.02
        return {'x': jax.random.normal(ks[0], (B, S, DM), dtype=jnp.float32), 'Wq': jax.random.normal(ks[1], (H * HD, DM), dtype=jnp.float32) * std, 'Wk': jax.random.normal(ks[2], (HKV * HD, DM), dtype=jnp.float32) * std, 'Wv': jax.random.normal(ks[3], (HKV * HD, DM), dtype=jnp.float32) * std, 'Wo': jax.random.normal(ks[4], (H * HD, DM), dtype=jnp.float32).T * (std / math.sqrt(2 * 32)), 'q_norm_w': jnp.ones((HD,), dtype=jnp.float32), 'k_norm_w': jnp.ones((HD,), dtype=jnp.float32)}
    _L0_attn_in = _L0_attn_setup()

    def _L0_ffn_setup():
        import jax, jax.numpy as jnp
        import numpy as np
        GROUP_SIZE = 128

        def dequantize(imatrix, scales, zeros, group_size, out_dtype):
            rs = jnp.repeat(scales, group_size, axis=0)
            rz = jnp.repeat(zeros, group_size, axis=0)
            return ((imatrix.astype(rs.dtype) - rz.astype(rs.dtype)) * rs).astype(out_dtype)
        key = jax.random.key(seed)
        ks = jax.random.split(key, 10)
        H, I, G = (512, 1792, GROUP_SIZE)
        B, S = (4, 256)
        x = jax.random.normal(ks[0], (B, S, H), dtype=jnp.float32)
        gate_w = jax.random.randint(ks[1], (H, I), 0, 16, dtype=jnp.int32)
        gate_z = jax.random.randint(ks[2], (H // G, I), 0, 16, dtype=jnp.int32)
        gate_s = jax.random.uniform(ks[3], (H // G, I), dtype=jnp.float32) * 0.01
        up_w = jax.random.randint(ks[4], (H, I), 0, 16, dtype=jnp.int32)
        up_z = jax.random.randint(ks[5], (H // G, I), 0, 16, dtype=jnp.int32)
        up_s = jax.random.uniform(ks[6], (H // G, I), dtype=jnp.float32) * 0.01
        down_w = jax.random.randint(ks[7], (I, H), 0, 16, dtype=jnp.int32)
        down_z = jax.random.randint(ks[8], (I // G, H), 0, 16, dtype=jnp.int32)
        down_s = jax.random.uniform(ks[9], (I // G, H), dtype=jnp.float32) * 0.01
        return {'x': x, 'gate_w': gate_w, 'gate_z': gate_z, 'gate_s': gate_s, 'up_w': up_w, 'up_z': up_z, 'up_s': up_s, 'down_w': down_w, 'down_z': down_z, 'down_s': down_s}
    _L0_ffn_in = _L0_ffn_setup()
    _d = {'L0_attn_x': _L0_attn_in['x'], 'L0_attn_Wq': _L0_attn_in['Wq'], 'L0_attn_Wk': _L0_attn_in['Wk'], 'L0_attn_Wv': _L0_attn_in['Wv'], 'L0_attn_Wo': _L0_attn_in['Wo'], 'L0_attn_q_norm_w': _L0_attn_in['q_norm_w'], 'L0_attn_k_norm_w': _L0_attn_in['k_norm_w'], 'L0_ffn_gate_w': _L0_ffn_in['gate_w'], 'L0_ffn_gate_z': _L0_ffn_in['gate_z'], 'L0_ffn_gate_s': _L0_ffn_in['gate_s'], 'L0_ffn_up_w': _L0_ffn_in['up_w'], 'L0_ffn_up_z': _L0_ffn_in['up_z'], 'L0_ffn_up_s': _L0_ffn_in['up_s'], 'L0_ffn_down_w': _L0_ffn_in['down_w'], 'L0_ffn_down_z': _L0_ffn_in['down_z'], 'L0_ffn_down_s': _L0_ffn_in['down_s']}
    _x0 = _d['L0_attn_x']
    _d['L0_attn_x'] = jax.random.normal(jax.random.fold_in(jax.random.key(seed), 1), (1, 1024, 512), dtype=_x0.dtype)
    del _x0
    return _d

def reference(L0_attn_x, L0_attn_Wq, L0_attn_Wk, L0_attn_Wv, L0_attn_Wo, L0_attn_q_norm_w, L0_attn_k_norm_w, L0_ffn_gate_w, L0_ffn_gate_z, L0_ffn_gate_s, L0_ffn_up_w, L0_ffn_up_z, L0_ffn_up_s, L0_ffn_down_w, L0_ffn_down_z, L0_ffn_down_s):

    def _L0_attn_ref(x, Wq, Wk, Wv, Wo, q_norm_w, k_norm_w):
        import jax, jax.numpy as jnp
        import numpy as np
        import math
        B, S, DM = (1, 256, 512)
        H, HKV, HD = (32, 8, 128)
        EPS = 1e-06
        NEG_INF = -1e+30

        def _alibi_slopes(n_heads: int) -> np.ndarray:
            start = 2 ** (-2 ** (-(math.log2(n_heads) - 3)))
            return np.array([start * start ** i for i in range(n_heads)], dtype=np.float32)

        def _rmsnorm(t, w):
            tf = t.astype(jnp.float32)
            inv = jax.lax.rsqrt(jnp.mean(tf * tf, axis=-1, keepdims=True) + EPS)
            return (tf * inv * w).astype(t.dtype)
        b, s, _ = x.shape
        G = H // HKV
        q = (x @ Wq.T).reshape(b, s, H, HD).transpose(0, 2, 1, 3)
        k = (x @ Wk.T).reshape(b, s, HKV, HD).transpose(0, 2, 1, 3)
        v = (x @ Wv.T).reshape(b, s, HKV, HD).transpose(0, 2, 1, 3)
        q = _rmsnorm(q, q_norm_w)
        k = _rmsnorm(k, k_norm_w)
        qg = q.reshape(b, HKV, G, s, HD)
        scores = jnp.einsum('bkgqd,bksd->bkgqs', qg, k) / math.sqrt(HD)
        slopes = jnp.asarray(_alibi_slopes(H)).reshape(HKV, G)
        pos = jnp.arange(s, dtype=jnp.float32)
        rel = pos[None, :] - pos[:, None]
        bias = jnp.where(rel > 0, NEG_INF, slopes[:, :, None, None] * rel)
        attn = jax.nn.softmax(scores + bias[None], axis=-1)
        out = jnp.einsum('bkgqs,bksd->bkgqd', attn, v)
        out = out.reshape(b, H, s, HD).transpose(0, 2, 1, 3).reshape(b, s, H * HD)
        return out @ Wo.T

    def _L0_ffn_ref(x, gate_w, gate_z, gate_s, up_w, up_z, up_s, down_w, down_z, down_s):
        import jax, jax.numpy as jnp
        import numpy as np
        GROUP_SIZE = 128

        def dequantize(imatrix, scales, zeros, group_size, out_dtype):
            rs = jnp.repeat(scales, group_size, axis=0)
            rz = jnp.repeat(zeros, group_size, axis=0)
            return ((imatrix.astype(rs.dtype) - rz.astype(rs.dtype)) * rs).astype(out_dtype)
        dt = x.dtype
        gate_proj = dequantize(gate_w, gate_s, gate_z, GROUP_SIZE, dt)
        up_proj = dequantize(up_w, up_s, up_z, GROUP_SIZE, dt)
        down_proj = dequantize(down_w, down_s, down_z, GROUP_SIZE, dt)
        gate = jax.nn.silu(jnp.dot(x, gate_proj))
        up = jnp.dot(x, up_proj)
        return jnp.dot(gate * up, down_proj)
    x = L0_attn_x
    xn = _layernorm(x, axis=-1)
    s = _L0_attn_ref(xn, L0_attn_Wq, L0_attn_Wk, L0_attn_Wv, L0_attn_Wo, L0_attn_q_norm_w, L0_attn_k_norm_w)
    g = _silu(_L0_ffn_ref(xn, L0_ffn_gate_w, L0_ffn_gate_z, L0_ffn_gate_s, L0_ffn_up_w, L0_ffn_up_z, L0_ffn_up_s, L0_ffn_down_w, L0_ffn_down_z, L0_ffn_down_s))
    x = x + s * g
    return x

_drawn_inputs = setup_inputs


def setup_inputs(seed=0):
    import zlib

    import numpy as np

    out = dict(_drawn_inputs(seed))
    spreads = {'L0_attn_q_norm_w': (1.0, 0.6), 'L0_attn_k_norm_w': (1.0, 0.6)}
    factors = {'L0_attn_Wq': 8.0,
     'L0_attn_Wk': 8.0,
     'L0_attn_Wv': 5.924,
     'L0_attn_Wo': 5.873,
     'L0_ffn_gate_s': 8.0,
     'L0_ffn_up_s': 8.0,
     'L0_ffn_down_s': 8.0}
    for name, (base, spread) in spreads.items():
        noise = np.random.default_rng([zlib.crc32(name.encode()), seed]).standard_normal(out[name].shape)
        drawn = base * np.exp(spread * noise) if base else spread * noise
        out[name] = jnp.asarray(drawn.astype(out[name].dtype))
    for name, factor in factors.items():
        out[name] = (out[name] * factor).astype(out[name].dtype)
    return out
```

```python
from contextlib import ExitStack

import numpy as np

import concourse.bass as bass
from concourse import mybir

F32 = mybir.dt.float32
F32R = mybir.dt.float32r
I32 = mybir.dt.int32
ALU = mybir.AluOpType
ACT = mybir.ActivationFunctionType

P = 128
TOK, DM = 1024, 512
HEADS, GROUPS, HD = 32, 8, 128
PER = HEADS // GROUPS
HID = 1792
QT = TOK // P
KT = DM // P
IT = HID // P
CH = 512
NC = TOK // CH
CT = CH // P
LN_EPS, RMS_EPS = 1e-5, 1e-6
MASKED = -1e30

TILES = list(range(QT - 1, -1, -1))
BASE = [P if t == 4 else 0 for t in range(QT)]
CUTS = [[(0, 256)], [(0, 256)], [(0, 384)], [(0, 512)], [(0, 384), (384, 256)], [(0, 512), (512, 256)],
        [(0, 512), (512, 384)], [(0, 512), (512, 512)]]
PBUF = [(0, 1024), (1024, 896), (1920, 768), (2688, 640)]
PBUF_COLS = 3328

STEP = 384
DIAG = [2048 + 1664, 2048]
PT_COLS = 2048 + 1664 + 4 * STEP + STEP


def pt_range(c, kt):
    r = kt - CT * c
    if r < 0:
        return kt * CH, CH, 0
    q0 = min(r, 2) * P
    return DIAG[c] + r * STEP + q0, CH - q0, q0


def parts(t):
    return [(0, 4), (4, t - 3)] if t >= CT else [(0, t + 1)]


PARTS = [(t, n) for t in TILES for n in range(len(parts(t)))]
LN_PARTS = QT


def part_no(h, t, n):
    return LN_PARTS + len(PARTS) * h + PARTS.index((t, n))


PRO = ["kv0", "kv1", "kv2", "kv3", "qc1_0", "ssc1_0"]


def group_order(first, last):
    out = []
    for j in range(PER):
        nx = (j + 1) % PER
        more = not (last and j == PER - 1)
        if j == 0:
            out += ["kt0", "kt1"] + ([] if first else ["v0_prev"]) + ["qc0_0", "ssc0_0"]
        else:
            out += [f"qc0_{j}", f"v0_{j - 1}", f"ssc0_{j}"]
        f1, f2 = [], []
        if j == 0 and not first:
            f1, f2 = [f"w{n}" for n in range(4)], [f"w{n}" for n in range(4, 8)]
        if j == PER - 1 and not last:
            f1, f2 = ["kv0", "kv1"], ["kv2", "kv3"]
        out += f1 + ([f"qc1_{nx}"] if more else []) + f2 + ([f"ssc1_{nx}"] if more else []) + [f"v1_{j}"]
    return out


FIRST, STEADY, LAST = group_order(True, False), group_order(False, False), group_order(False, True)
EPI = ["v0_prev"] + [f"w{n}" for n in range(8)]


def split_by_act(name):
    return name[0] in "vq" or name[:2] == "kt" or name[:2] == "v0"


class Places:

    def __init__(self, kind, g=None):
        self.order = {"pro": PRO, "first": FIRST, "steady": STEADY, "last": LAST, "epi": EPI}[kind]
        hi = lambda names: sum(map(split_by_act, names))
        a, b = len(PRO), hi(PRO)
        if kind == "pro":
            self.a, self.b, self.parity = 0, 0, 0
            return
        if kind == "first":
            self.a, self.b, self.parity = a, b, a % 2
            return
        a, b = a + len(FIRST), b + hi(FIRST)
        self.parity = a % 2
        if kind == "epi":
            self.a, self.b = a + len(STEADY) * (GROUPS - 2) + len(LAST), b + hi(STEADY) * (GROUPS - 2) + hi(LAST)
            self.parity = self.a % 2
            return
        n, m = len(STEADY), hi(STEADY)
        self.a, self.b = g * n + (a - n), g * m + (b - m)

    def n(self, name, more=1):
        return self.a + (self.order.index(name) + more)

    def hi(self, name):
        i = self.order.index(name)
        return self.b + sum(map(split_by_act, self.order[:i + 1]))

    def bank(self, name):
        return (self.parity + self.order.index(name)) % 2


assert len(STEADY) % 2 == 0


def f(ap):
    return ap.bitcast(F32)


def attention(nc, stack, keep, x, wq, wkv, wo, slopes, qkw):
    sb = lambda n, shape, dt=F32: stack.enter_context(nc.sbuf_tensor(n, shape, dt))
    sem = lambda n: stack.enter_context(nc.semaphore(n))
    xh, xl, s_acc = keep["xh"], keep["xl"], keep["s"]
    xs = s_acc[:, :].rearrange("p (i n) -> p i n", i=QT)
    sT = s_acc[:, :].rearrange("p (m n) -> p m n", m=KT)

    pt_h, pt_l = sb("pt_h", [P, PT_COLS], F32R), sb("pt_l", [P, PT_COLS], F32R)
    oT_h, oT_l = sb("oT_h", [P, PER, TOK], F32R), sb("oT_l", [P, PER, TOK], F32R)
    kT_h, kT_l = sb("kT_h", [P, TOK], F32R), sb("kT_l", [P, TOK], F32R)
    v_h, v_l = sb("v_h", [P, QT, HD], F32R), sb("v_l", [P, QT, HD], F32R)
    q_h, q_l = sb("q_h", [P, TOK], F32R), sb("q_l", [P, TOK], F32R)
    wq_h, wq_l = sb("wq_h", [P, KT, HD], F32R), sb("wq_l", [P, KT, HD], F32R)
    wkv_h, wkv_l = sb("wkv_h", [P, KT, 2 * HD], F32R), sb("wkv_l", [P, KT, 2 * HD], F32R)
    wo_h, wo_l = sb("wo_h", [P, PER, DM], F32R), sb("wo_l", [P, PER, DM], F32R)
    wq_in, wkv_in, wo_in = sb("wq_in", [P, KT, HD]), sb("wkv_in", [P, KT, 2 * HD]), sb("wo_in", [P, DM])
    kv = sb("kv", [P, QT, 2 * HD])
    sq = sb("sq", [P, TOK])
    pb = sb("pb", [P, PBUF_COLS])
    rel = sb("rel", [P, TOK])
    junk = sb("junk", [P, HD])
    ident = sb("ident", [P, P])
    ones = sb("ones", [P, QT])
    sl = sb("sl", [P, HEADS])
    qk_w = sb("qk_w", [P, 2])
    qk = sb("qk", [P, 1])
    cst = sb("cst", [P, 3])
    stats = sb("stats", [P, QT, 6])
    mv = sb("mv", [P, QT, 2])
    var_e = sb("var_e", [P, QT])
    rstd = sb("rstd", [P, QT])
    kss, kms, kinv = sb("kss", [P, QT]), sb("kms", [P, QT]), sb("kinv", [P, QT])
    ms, root, inv, ninv, coef = (sb(n, [P, QT]) for n in ("ms", "root", "inv", "ninv", "coef"))
    low, rsum, rinv = sb("low", [P, QT]), sb("rsum", [P, QT]), sb("rinv", [P, QT])

    S = [stack.enter_context(nc.psum_tensor(f"S{n}", [P, 2 * CH], F32)) for n in range(2)]
    T = [stack.enter_context(nc.psum_tensor(f"T{n}", [P, CH], F32)) for n in range(2)]
    O = [stack.enter_context(nc.psum_tensor(f"O{n}", [P, CH], F32)) for n in range(2)]

    x_in, tab_in = sem("x_in"), sem("tab_in")
    wq_ld, wkv_ld, wo_ld = sem("wq_ld"), sem("wkv_ld"), sem("wo_ld")
    wq_split, wkv_split, wo_split = sem("wq_split"), sem("wkv_split"), sem("wo_split")
    setup, ln, ln_var, ln_rstd, xn_ready = sem("setup"), sem("ln"), sem("ln_var"), sem("ln_rstd"), sem("xn_ready")
    sT_zero, qk_ready = sem("sT_zero"), sem("qk_ready")
    tr_ready, tr_hi, tr_lo = sem("tr_ready"), sem("tr_hi"), sem("tr_lo")
    out_ready, out_hi, out_free = sem("out_ready"), sem("out_hi"), sem("out_free")
    kss_ready, kms_ready, kinv_ready, kn_ready, v_ready = (
        sem("kss_ready"), sem("kms_ready"), sem("kinv_ready"), sem("kn_ready"), sem("v_ready"))
    root_ready, coef_ready = sem("root_ready"), sem("coef_ready")
    bias_ready, scores_ready, logits_ready = sem("bias_ready"), sem("scores_ready"), sem("logits_ready")
    exps_ready, rinv_ready, probs_ready = sem("exps_ready"), sem("rinv_ready"), sem("probs_ready")
    wsp = sem("wsp")
    SETUP = 7

    def pbuf(idx, t):
        a, w = PBUF[idx % 4]
        return pb[:, a:a + (t + 1) * P]

    def pt_lot(pt, t, n):
        k0, m = parts(t)[n]
        c, ql = t // CT, t % CT
        if k0 == 0 and c == 1:
            return pt[:, 0:4 * CH].rearrange("p (k w) -> p k w", w=CH)[:, :, ql * P:(ql + 1) * P]
        a = DIAG[c] + ql * P
        return pt[:, a:a + m * STEP].rearrange("p (k w) -> p k w", w=STEP)[:, :, 0:P]

    block = stack.enter_context(nc.Block())

    @block.sync
    def _(sp):
        for i in range(QT):
            sp.dma_start(xs[:, i, :], x[i]).then_inc(x_in, 16)
        sp.dma_start(wkv_in[:, :, :], wkv[0]).then_inc(wkv_ld, 16)
        sp.dma_start(wq_in[:, :, :], wq[0]).then_inc(wq_ld, 16)
        sp.dma_start(sl[:, :], slopes).then_inc(tab_in, 16)
        sp.dma_start(qk_w[:, :], qkw).then_inc(tab_in, 16)
        sp.dma_start(wo_in[:, :], wo[0]).then_inc(wo_ld, 16)

        def group(g, last=False):
            if not last:
                sp.wait_ge(wkv_split, g * 2 + 2)
                sp.dma_start(wkv_in[:, :, :], wkv[g + 1]).then_inc(wkv_ld, 16)
            for j in range(PER):
                h = g * PER + j
                if not (last and j == PER - 1):
                    sp.wait_ge(wq_split, h * 2 + 2)
                    sp.dma_start(wq_in[:, :, :], wq[h + 1]).then_inc(wq_ld, 16)
                    if j > 0:
                        sp.wait_ge(wo_split, h * 2)
                        sp.dma_start(wo_in[:, :], wo[h]).then_inc(wo_ld, 16)
                if j == PER - 1:
                    if last:
                        sp.wait_ge(wo_split, h * 2)
                        sp.dma_start(wo_in[:, :], wo[h]).then_inc(wo_ld, 16)
                    else:
                        sp.wait_ge(wo_split, h * 2 + 2)
                        sp.dma_start(wo_in[:, :], wo[h + 1]).then_inc(wo_ld, 16)

        group(0)
        with sp.Fori(1, GROUPS - 1) as g:
            group(g)
        group(GROUPS - 1, last=True)

    @block.gpsimd
    def _(pool):
        g_ = nc.gpsimd
        g_.memset(ones[:, :], 1.0).then_inc(setup, 1)
        g_.memset(cst[:, 0:1], -0.5).then_inc(setup, 1)
        g_.memset(cst[:, 1:2], 0.5).then_inc(setup, 1)
        g_.memset(cst[:, 2:3], -1.0).then_inc(setup, 1)
        g_.memset(ident[:, :], 0.0).then_inc(setup, 1)
        g_.iota(rel[:, :], pattern=[[1, TOK]], base=-(TOK - P), channel_multiplier=-1,
                allow_small_or_imprecise_dtypes=True).then_inc(setup, 1)
        pool.wait_ge(setup, 6)
        g_.affine_select(out=ident[:, :], in_=ident[:, :], compare_op=ALU.not_equal, fill=1.0, base=0,
                         pattern=[[-1, P]], channel_multiplier=1).then_inc(setup, 1)
        g_.affine_select(out=rel[:, :], in_=rel[:, :], compare_op=ALU.is_ge, fill=MASKED, base=TOK - P,
                         pattern=[[-1, TOK]], channel_multiplier=1).then_inc(setup, 1)
        for c in range(NC):
            a, _, _ = pt_range(c, CT * c + 3)
            for pt in (pt_h, pt_l):
                g_.memset(f(pt[:, a:a + P]), 0.0).then_inc(setup, 1)

        def split(hi, lo, src, done, n):
            if len(src.shape) == 3:
                one = ones[:, 0:src.shape[1]].rearrange("p (k o) -> p k o", o=1).to_broadcast(list(src.shape))
            else:
                one = ones[:, 0:1].to_broadcast(list(src.shape))
            g_.tensor_tensor(hi, src, one, ALU.mult).then_inc(done, 1)
            pool.wait_ge(done, n + 1)
            g_.tensor_tensor(lo, src, f(hi), ALU.subtract).then_inc(done, 1)

        def split_wq(h, at=None, before=None):
            pool.wait_ge(wq_ld, h * 16 + 16)
            if at is not None:
                pool.wait_ge(out_ready, at.n(before))
            split(wq_h[:, :, :], wq_l[:, :, :], wq_in[:, :, :], wq_split, h * 2)

        def split_wkv(g, at=None):
            pool.wait_ge(wkv_ld, g * 16 + 16)
            split(wkv_h[:, :, :], wkv_l[:, :, :], wkv_in[:, :, :], wkv_split, g * 2)

        def split_wo(h, hh, at=None):
            pool.wait_ge(wo_ld, h * 16 + 16)
            if at is not None:
                pool.wait_ge(out_ready, at.n("w7"))
            split(wo_h[:, hh, :], wo_l[:, hh, :], wo_in[:, :], wo_split, h * 2)

        def norms(h, c, ready, value):
            cs = slice(c * CT, (c + 1) * CT)
            n = h * 2 + (1 - c)
            pool.wait_ge(out_free, value)
            half = lambda k: cst[:, k:k + 1].to_broadcast([P, CT])
            g_.tensor_tensor(root[:, cs], ms[:, cs], half(1), ALU.pow).then_inc(root_ready, 1)
            g_.tensor_tensor(inv[:, cs], ms[:, cs], half(0), ALU.pow).then_inc(root_ready, 1)
            pool.wait_ge(root_ready, n * 2 + 2)
            g_.tensor_tensor(ninv[:, cs], inv[:, cs], half(2), ALU.mult).then_inc(coef_ready, 1)
            slope = sl[:, bass.ds(h, 1)] if not isinstance(h, int) else sl[:, h:h + 1]
            g_.tensor_tensor(coef[:, cs], root[:, cs], slope.to_broadcast([P, CT]),
                             ALU.mult).then_inc(coef_ready, 1)

        def bias(h, idx):
            t = TILES[idx]
            c = t // CT
            pool.wait_ge(coef_ready, h * 4 + (2 - c) * 2)
            if idx < 4:
                if not (isinstance(h, int) and h == 0):
                    prev = TILES[idx + 4]
                    pool.wait_ge(tr_ready, part_no(h - 1, prev, len(parts(prev)) - 1) + 1)
            else:
                prev = TILES[idx - 4]
                pool.wait_ge(tr_ready, part_no(h, prev, len(parts(prev)) - 1) + 1)
            w = (t + 1) * P
            g_.tensor_tensor(pbuf(idx, t), rel[:, TOK - w:TOK], coef[:, t:t + 1].to_broadcast([P, w]),
                             ALU.mult).then_inc(bias_ready, 1)

        def normalise(h, idx):
            t = TILES[idx]
            w = (t + 1) * P
            pool.wait_ge(rinv_ready, h * QT + (idx + 1))
            g_.tensor_tensor(pbuf(idx, t), pbuf(idx, t), rinv[:, idx:idx + 1].to_broadcast([P, w]),
                             ALU.mult).then_inc(probs_ready, 1)

        def k_norm(g):
            pool.wait_ge(kms_ready, g + 1)
            g_.tensor_tensor(kinv[:, :], kms[:, :], cst[:, 0:1].to_broadcast([P, QT]),
                             ALU.pow).then_inc(kinv_ready, 1)
            pool.wait_ge(kinv_ready, g + 1)
            g_.tensor_tensor(kv[:, :, 0:HD], kv[:, :, 0:HD],
                             kinv[:, :].rearrange("p (k o) -> p k o", o=1).to_broadcast([P, QT, HD]),
                             ALU.mult).then_inc(kn_ready, 1)

        pool.wait_ge(setup, SETUP + 5)
        pool.wait_ge(ln_var, 1)
        g_.tensor_tensor(rstd[:, :], var_e[:, :], cst[:, 0:1].to_broadcast([P, QT]), ALU.pow).then_inc(ln_rstd, 1)
        split_wkv(0)
        split_wq(0)
        pool.wait_ge(tr_ready, LN_PARTS)
        g_.memset(s_acc[:, :], 0.0).then_inc(sT_zero, 1)
        pool.wait_ge(tab_in, 32)
        norms(0, 1, out_free, Places("pro").n("ssc1_0"))
        bias(0, 0)
        bias(0, 1)
        k_norm(0)

        def group(g, kind):
            at = Places(kind, g)
            last = kind == "last"
            if kind != "first":
                pool.wait_ge(out_ready, at.n("v0_prev"))
            split(v_h[:, :, :], v_l[:, :, :], kv[:, :, HD:2 * HD], v_ready, g * 2)
            for j in range(PER):
                h = g * PER + j
                more = not (last and j == PER - 1)
                for idx in range(QT):
                    normalise(h, idx)
                    if idx + 2 < QT:
                        bias(h, idx + 2)
                    elif more:
                        bias(h + 1, idx + 2 - QT)
                    if idx == 0:
                        norms(h, 0, out_free, at.n(f"ssc0_{j}"))
                    if idx == 1 and more:
                        split_wq(h + 1, at, f"qc0_{j}")
                    if idx == 2 and j == 2 and not last:
                        split_wkv(g + 1)
                    if idx == 3 and more:
                        norms(h + 1, 1, out_free, at.n(f"ssc1_{(j + 1) % PER}"))
                    if idx == 6 and j == PER - 1 and not last:
                        k_norm(g + 1)
                    if idx == 5 and j > 0:
                        split_wo(g * PER + j - 1, j - 1, None if kind == "first" else at)
                        if j == PER - 1:
                            split_wo(g * PER + j, j, None if kind == "first" else at)

        group(0, "first")
        with pool.Fori(1, GROUPS - 1) as g:
            group(g, "steady")
        group(GROUPS - 1, "last")

    @block.scalar
    def _(act):
        a_ = nc.scalar

        def lot(h, t, n):
            no = part_no(h, t, n)
            m = parts(t)[n][1]
            act.wait_ge(tr_ready, no + 1)
            bank = T[PARTS.index((t, n)) % 2]
            a_.activation(pt_lot(pt_h, t, n), bank[:, 0:m * P].rearrange("p (k w) -> p k w", w=P),
                          ACT.Copy).then_inc(tr_hi, 1)

        def lots(h, t):
            for n in range(len(parts(t))):
                lot(h, t, n)

        def exp(h, idx):
            t = TILES[idx]
            act.wait_ge(logits_ready, h * QT + (idx + 1))
            a_.activation(pbuf(idx, t), pbuf(idx, t), ACT.Exp, bias=low[:, idx:idx + 1], scale=-1.0,
                          accum_out=rsum[:, idx:idx + 1]).then_inc(exps_ready, 1)

        def q_hi(at, name):
            cs = slice(CH * (name[2] == "1"), CH * (name[2] == "1") + CH)
            act.wait_ge(out_ready, at.n(name))
            a_.activation(q_h[:, cs], O[at.bank(name)][:, :], ACT.Copy)
            a_.activation(sq[:, cs], O[at.bank(name)][:, :], ACT.Square).then_inc(out_hi, 1)

        def v_hi(at, name, j):
            cs = slice(CH * (name[1] == "1"), CH * (name[1] == "1") + CH)
            act.wait_ge(out_ready, at.n(name))
            a_.activation(oT_h[:, j, cs], O[at.bank(name)][:, :], ACT.Copy).then_inc(out_hi, 1)

        def k_squares(at, names, g):
            for name in names:
                act.wait_ge(out_free, at.n(name))
                for k in (2 * int(name[2]), 2 * int(name[2]) + 1):
                    if not (isinstance(g, int) and g * QT + k == 0):
                        act.wait_ge(kss_ready, g * QT + k)
                    a_.activation(junk[:, :], kv[:, k, 0:HD], ACT.Square,
                                  accum_out=kss[:, k:k + 1]).then_inc(kss_ready, 1)

        for i in range(QT):
            act.wait_ge(tr_ready, i + 1)
            a_.activation(xh[:, :, i * P:(i + 1) * P], T[i % 2][:, :].rearrange("p (k w) -> p k w", w=P),
                          ACT.Copy).then_inc(tr_hi, 1)
        pro = Places("pro")
        k_squares(pro, ["kv0", "kv1", "kv2", "kv3"], 0)
        q_hi(pro, "qc1_0")

        def group(g, kind):
            at = Places(kind, g)
            act.wait_ge(qk_ready, 1)
            for n in range(2):
                act.wait_ge(out_ready, at.n(f"kt{n}"))
                a_.activation(kT_h[:, n * CH:(n + 1) * CH], O[at.bank(f"kt{n}")][:, :], ACT.Copy,
                              scale=qk[:, 0:1]).then_inc(out_hi, 1)
            for j in range(PER):
                h = g * PER + j
                more = not (kind == "last" and j == PER - 1)
                if j == 0:
                    if kind != "first":
                        lots(h - 1, 1)
                        lots(h - 1, 0)
                        v_hi(at, "v0_prev", PER - 1)
                    exp(h, 0)
                else:
                    exp(h, 0)
                    lots(h - 1, 1)
                    lots(h - 1, 0)
                q_hi(at, f"qc0_{j}")
                exp(h, 1)
                if j > 0:
                    v_hi(at, f"v0_{j - 1}", j - 1)
                lots(h, 7)
                exp(h, 2)
                lots(h, 6)
                exp(h, 3)
                if more:
                    if j == PER - 1:
                        k_squares(at, ["kv0", "kv1"], g + 1)
                    q_hi(at, f"qc1_{(j + 1) % PER}")
                lots(h, 5)
                exp(h, 4)
                lots(h, 4)
                exp(h, 5)
                exp(h, 6)
                if more and j == PER - 1:
                    k_squares(at, ["kv2", "kv3"], g + 1)
                v_hi(at, f"v1_{j}", j)
                lots(h, 3)
                lots(h, 2)
                exp(h, 7)

        group(0, "first")
        with act.Fori(1, GROUPS - 1) as g:
            group(g, "steady")
        group(GROUPS - 1, "last")
        lots(HEADS - 1, 1)
        lots(HEADS - 1, 0)
        v_hi(Places("epi"), "v0_prev", PER - 1)

    @block.vector
    def _(dve):
        v_ = nc.vector
        for i in range(QT):
            dve.wait_ge(x_in, 16 * QT)
            v_.bn_stats(stats[:, i, :], xs[:, i, :]).then_inc(ln, 1)
        for i in range(QT):
            dve.wait_ge(ln, i + 1)
            v_.bn_aggr(mv[:, i, :], stats[:, i, :]).then_inc(ln, 1)
        dve.wait_ge(ln, 2 * QT)
        v_.tensor_scalar(var_e[:, :], mv[:, :, 1], LN_EPS, None, ALU.add).then_inc(ln_var, 1)
        dve.wait_ge(ln_rstd, 1)
        for i in range(QT):
            v_.tensor_scalar(xs[:, i, :], xs[:, i, :], mv[:, i, 0:1], rstd[:, i:i + 1], ALU.subtract,
                             ALU.mult).then_inc(xn_ready, 1)
        dve.wait_ge(tab_in, 32)
        v_.tensor_tensor(qk[:, :], qk_w[:, 0:1], qk_w[:, 1:2], ALU.mult).then_inc(qk_ready, 1)
        for i in range(QT):
            dve.wait_ge(tr_hi, i + 1)
            cs = slice(i * P, (i + 1) * P)
            v_.tensor_tensor(xl[:, :, cs], T[i % 2][:, :].rearrange("p (k w) -> p k w", w=P), f(xh[:, :, cs]),
                             ALU.subtract).then_inc(tr_lo, 1)

        def lots(h, t):
            for n in range(len(parts(t))):
                m = parts(t)[n][1]
                dve.wait_ge(tr_hi, part_no(h, t, n) + 1)
                bank = T[PARTS.index((t, n)) % 2]
                v_.tensor_tensor(pt_lot(pt_l, t, n), bank[:, 0:m * P].rearrange("p (k w) -> p k w", w=P),
                                 f(pt_lot(pt_h, t, n)), ALU.subtract).then_inc(tr_lo, 1)

        def logits(h, idx):
            t = TILES[idx]
            n = h * QT + (idx + 1)
            dve.compute_val(n)
            dve.wait_ge(setup, SETUP + 5)
            dve.wait_ge(bias_ready, n)
            dve.wait_ge(scores_ready, n)
            v_.tensor_tensor_reduce(out=pbuf(idx, t), in0=S[idx % 2][:, BASE[t]:BASE[t] + (t + 1) * P],
                                    in1=pbuf(idx, t), scale=ninv[:, t:t + 1], scalar=3e38, op0=ALU.add,
                                    op1=ALU.min, accum_out=low[:, idx:idx + 1]).then_inc(logits_ready, 1)

        def recip(h, idx):
            dve.wait_ge(exps_ready, h * QT + (idx + 1))
            v_.reciprocal(rinv[:, idx:idx + 1], rsum[:, idx:idx + 1]).then_inc(rinv_ready, 1)

        def q_lo(at, name):
            cs = slice(CH * (name[2] == "1"), CH * (name[2] == "1") + CH)
            dve.wait_ge(out_hi, at.hi(name))
            v_.tensor_tensor(q_l[:, cs], O[at.bank(name)][:, :], f(q_h[:, cs]), ALU.subtract).then_inc(out_free, 1)

        def v_lo(at, name, j):
            cs = slice(CH * (name[1] == "1"), CH * (name[1] == "1") + CH)
            dve.wait_ge(out_hi, at.hi(name))
            v_.tensor_tensor(oT_l[:, j, cs], O[at.bank(name)][:, :], f(oT_h[:, j, cs]),
                             ALU.subtract).then_inc(out_free, 1)

        def mean_sq(at, name):
            cs = slice(CT * (name[3] == "1"), CT * (name[3] == "1") + CT)
            dve.wait_ge(out_ready, at.n(name))
            v_.tensor_scalar(ms[:, cs], O[at.bank(name)][:, 0:CT], HD * RMS_EPS, None,
                             ALU.add).then_inc(out_free, 1)

        def kv_copy(at, names, g):
            for name in names:
                k = 2 * int(name[2])
                dve.wait_ge(v_ready, g * 2)
                dve.wait_ge(out_ready, at.n(name))
                v_.tensor_copy(kv[:, k:k + 2, :], O[at.bank(name)][:, :].rearrange("p (k w) -> p k w", w=2 * HD)
                               ).then_inc(out_free, 1)

        def k_mean_sq(g):
            dve.wait_ge(kss_ready, g * QT + QT)
            v_.tensor_scalar(kms[:, :], kss[:, :], 1.0 / HD, RMS_EPS, ALU.mult, ALU.add).then_inc(kms_ready, 1)

        def project(at, names):
            for name in names:
                m, c = divmod(int(name[1]), NC)
                dst = sT[:, m, c * CH:(c + 1) * CH]
                dve.wait_ge(out_ready, at.n(name))
                v_.tensor_tensor(dst, O[at.bank(name)][:, :], dst, ALU.add).then_inc(out_free, 1)

        pro = Places("pro")
        for n in range(4):
            dve.wait_ge(out_ready, pro.n(f"kv{n}"))
            v_.tensor_copy(kv[:, 2 * n:2 * n + 2, :], O[pro.bank(f"kv{n}")][:, :].rearrange("p (k w) -> p k w", w=2 * HD)
                           ).then_inc(out_free, 1)
        q_lo(pro, "qc1_0")
        mean_sq(pro, "ssc1_0")
        k_mean_sq(0)
        dve.wait_ge(sT_zero, 1)

        def group(g, kind):
            at = Places(kind, g)
            last = kind == "last"
            for n in range(2):
                cs = slice(n * CH, (n + 1) * CH)
                dve.wait_ge(out_hi, at.hi(f"kt{n}"))
                v_.scalar_tensor_tensor(out=kT_l[:, cs], in0=O[at.bank(f"kt{n}")][:, :], scalar=qk[:, 0:1],
                                        in1=f(kT_h[:, cs]), op0=ALU.mult, op1=ALU.subtract).then_inc(out_free, 1)
            for j in range(PER):
                h = g * PER + j
                nx = (j + 1) % PER
                more = not (last and j == PER - 1)
                prev = not (kind == "first" and j == 0)
                if j == 0:
                    if prev:
                        recip(h - 1, 7)
                        lots(h - 1, 1)
                        lots(h - 1, 0)
                        v_lo(at, "v0_prev", PER - 1)
                    logits(h, 0)
                else:
                    logits(h, 0)
                    recip(h - 1, 7)
                    lots(h - 1, 1)
                    lots(h - 1, 0)
                q_lo(at, f"qc0_{j}")
                recip(h, 0)
                logits(h, 1)
                if j > 0:
                    v_lo(at, f"v0_{j - 1}", j - 1)
                mean_sq(at, f"ssc0_{j}")
                recip(h, 1)
                lots(h, 7)
                logits(h, 2)
                if j == 0 and kind != "first":
                    project(at, ["w0", "w1", "w2", "w3"])
                if j == PER - 1 and not last:
                    kv_copy(at, ["kv0", "kv1"], g + 1)
                lots(h, 6)
                recip(h, 2)
                logits(h, 3)
                if more:
                    q_lo(at, f"qc1_{nx}")
                recip(h, 3)
                lots(h, 5)
                logits(h, 4)
                if j == 0 and kind != "first":
                    project(at, ["w4", "w5", "w6", "w7"])
                if j == PER - 1 and not last:
                    kv_copy(at, ["kv2", "kv3"], g + 1)
                if more:
                    mean_sq(at, f"ssc1_{nx}")
                recip(h, 4)
                lots(h, 4)
                logits(h, 5)
                logits(h, 6)
                recip(h, 5)
                v_lo(at, f"v1_{j}", j)
                recip(h, 6)
                lots(h, 3)
                lots(h, 2)
                logits(h, 7)
            if not last:
                k_mean_sq(g + 1)

        group(0, "first")
        with dve.Fori(1, GROUPS - 1) as g:
            group(g, "steady")
        group(GROUPS - 1, "last")
        recip(HEADS - 1, 7)
        lots(HEADS - 1, 1)
        lots(HEADS - 1, 0)
        epi = Places("epi")
        v_lo(epi, "v0_prev", PER - 1)
        project(epi, [f"w{n}" for n in range(8)])

    @block.tensor
    def _(pe):
        mm = nc.tensor.matmul

        def products(out, terms):
            n = 0
            for ah, al, bh, bl in terms:
                for a, b in ((ah, bh), (ah, bl), (al, bh)):
                    ins = mm(out, a, b, start=(n == 0), stop=(n == 3 * len(terms) - 1))
                    n += 1
            return ins

        def take(at, name):
            first2 = at.order is PRO and at.order.index(name) < 2
            if not first2:
                pe.wait_ge(out_free, at.n(name, more=-1))
            return O[at.bank(name)]

        def lots(h, t):
            idx = TILES.index(t)
            pe.wait_ge(probs_ready, h * QT + (idx + 1))
            for n, (k0, m) in enumerate(parts(t)):
                no = part_no(h, t, n)
                pe.wait_ge(tr_lo, no - 1)
                bank = T[PARTS.index((t, n)) % 2]
                for k in range(m):
                    ins = nc.tensor.transpose(bank[:, k * P:(k + 1) * P],
                                              pbuf(idx, t)[:, (k0 + k) * P:(k0 + k + 1) * P], ident[:, :])
                ins.then_inc(tr_ready, 1)

        def scores(h, idx):
            t = TILES[idx]
            if not (isinstance(h, int) and h == 0 and idx < 2):
                pe.wait_ge(logits_ready, h * QT + (idx - 1))
            bank = S[idx % 2]
            qs = slice(t * P, (t + 1) * P)
            cuts = CUTS[t]
            for q, last in ((q_h, False), (q_l, True)):
                for k0, w in cuts:
                    out = bank[:, BASE[t] + k0:BASE[t] + k0 + w]
                    if not last:
                        mm(out, q[:, qs], kT_h[:, k0:k0 + w], start=True, stop=False)
                        mm(out, q[:, qs], kT_l[:, k0:k0 + w], start=False, stop=False)
                    else:
                        ins = mm(out, q[:, qs], kT_h[:, k0:k0 + w], start=False, stop=True)
            ins.then_inc(scores_ready, 1)

        def values(at, name, h, wait):
            c = int(name[1])
            out = take(at, name)
            last_t = TILES[TILES.index(c * CT)]
            pe.wait_ge(tr_lo, part_no(h, last_t, len(parts(last_t)) - 1) + 1)
            if wait is not None:
                pe.wait_ge(v_ready, wait)
            n = CT * (c + 1)
            for kt in range(n):
                a, w, q0 = pt_range(c, kt)
                o = out[:, q0:q0 + w]
                mm(o, v_h[:, kt, :], pt_h[:, a:a + w], start=(kt == 0), stop=False)
                mm(o, v_h[:, kt, :], pt_l[:, a:a + w], start=False, stop=False)
                ins = mm(o, v_l[:, kt, :], pt_h[:, a:a + w], start=False, stop=(kt == n - 1))
            ins.then_inc(out_ready, 1)

        def q_proj(at, name, h):
            c = int(name[2])
            out = take(at, name)
            pe.wait_ge(wq_split, h * 2 + 2)
            cs = slice(c * CH, (c + 1) * CH)
            products(out[:, :], [(wq_h[:, k, :], wq_l[:, k, :], xh[:, k, cs], xl[:, k, cs]) for k in range(KT)]
                     ).then_inc(out_ready, 1)

        def sums(at, name, of):
            c = int(name[3])
            out = take(at, name)
            pe.wait_ge(out_free, at.n(of))
            for i in range(CT):
                a = (c * CT + i) * P
                ins = mm(out[:, i:i + 1], sq[:, a:a + P], ones[:, 0:1], start=True, stop=True)
            ins.then_inc(out_ready, 1)

        def kv_proj(at, names, g):
            for name in names:
                out = take(at, name)
                pe.wait_ge(wkv_split, g * 2 + 2)
                for i in range(2):
                    a = (2 * int(name[2]) + i) * P
                    ins = products(out[:, i * 2 * HD:(i + 1) * 2 * HD],
                                   [(xh[:, k, a:a + P], xl[:, k, a:a + P], wkv_h[:, k, :], wkv_l[:, k, :])
                                    for k in range(KT)])
                ins.then_inc(out_ready, 1)

        def k_transposes(at, g):
            pe.wait_ge(kn_ready, g + 1)
            for n in range(2):
                out = take(at, f"kt{n}")
                for i in range(4):
                    ins = nc.tensor.transpose(out[:, i * P:(i + 1) * P], kv[:, 4 * n + i, 0:HD], ident[:, :])
                ins.then_inc(out_ready, 1)

        def project(at, names, h0):
            for name in names:
                m, c = divmod(int(name[1]), NC)
                out = take(at, name)
                pe.wait_ge(wo_split, h0 * 2 + 8)
                pe.wait_ge(out_free, at.n("v0_prev"))
                ms_, cs = slice(m * P, (m + 1) * P), slice(c * CH, (c + 1) * CH)
                products(out[:, :], [(wo_h[:, j, ms_], wo_l[:, j, ms_], oT_h[:, j, cs], oT_l[:, j, cs])
                                     for j in range(PER)]).then_inc(out_ready, 1)

        pe.wait_ge(setup, SETUP + 5)
        for i in range(QT):
            pe.wait_ge(xn_ready, i + 1)
            if i >= 2:
                pe.wait_ge(tr_lo, i - 1)
            for k in range(KT):
                ins = nc.tensor.transpose(T[i % 2][:, k * P:(k + 1) * P], xs[:, i, k * P:(k + 1) * P], ident[:, :])
            ins.then_inc(tr_ready, 1)
        pro = Places("pro")
        pe.wait_ge(tr_lo, LN_PARTS)
        kv_proj(pro, ["kv0", "kv1", "kv2", "kv3"], 0)
        q_proj(pro, "qc1_0", 0)
        sums(pro, "ssc1_0", "qc1_0")

        def group(g, kind):
            at = Places(kind, g)
            last = kind == "last"
            k_transposes(at, g)
            for j in range(PER):
                h = g * PER + j
                nx = (j + 1) % PER
                more = not (last and j == PER - 1)
                if j == 0:
                    if kind != "first":
                        lots(h - 1, 1)
                        lots(h - 1, 0)
                        values(at, "v0_prev", h - 1, None)
                    pe.wait_ge(out_free, at.n("kt1"))
                    scores(h, 0)
                else:
                    scores(h, 0)
                    lots(h - 1, 1)
                    lots(h - 1, 0)
                q_proj(at, f"qc0_{j}", h)
                scores(h, 1)
                if j > 0:
                    values(at, f"v0_{j - 1}", h - 1, None)
                sums(at, f"ssc0_{j}", f"qc0_{j}")
                lots(h, 7)
                scores(h, 2)
                if j == 0 and kind != "first":
                    project(at, ["w0", "w1", "w2", "w3"], h - PER)
                if j == PER - 1 and not last:
                    kv_proj(at, ["kv0", "kv1"], g + 1)
                lots(h, 6)
                scores(h, 3)
                if more:
                    q_proj(at, f"qc1_{nx}", h + 1)
                lots(h, 5)
                scores(h, 4)
                if j == 0 and kind != "first":
                    project(at, ["w4", "w5", "w6", "w7"], h - PER)
                if j == PER - 1 and not last:
                    kv_proj(at, ["kv2", "kv3"], g + 1)
                if more:
                    sums(at, f"ssc1_{nx}", f"qc1_{nx}")
                lots(h, 4)
                scores(h, 5)
                scores(h, 6)
                values(at, f"v1_{j}", h, g * 2 + 2 if j == 0 else None)
                lots(h, 3)
                lots(h, 2)
                scores(h, 7)

        group(0, "first")
        with pe.Fori(1, GROUPS - 1) as g:
            group(g, "steady")
        group(GROUPS - 1, "last")
        lots(HEADS - 1, 1)
        lots(HEADS - 1, 0)
        epi = Places("epi")
        values(epi, "v0_prev", HEADS - 1, None)
        project(epi, [f"w{n}" for n in range(8)], HEADS - PER)


def ffn(nc, stack, keep, xT, mats, down_sc, outT):
    sb = lambda n, shape, dt=F32: stack.enter_context(nc.sbuf_tensor(n, shape, dt))
    sem = lambda n: stack.enter_context(nc.semaphore(n))
    xh, xl = keep["xh"], keep["xl"]
    sT = keep["s"][:, :].rearrange("p (m n) -> p m n", m=KT)
    yT = sb("yT", [P, KT, TOK])
    xt = sb("xt", [P, KT, TOK])
    KIND = ("gate", "up", "down")
    w_in = {k: sb(f"{k}_in", [P, CH], I32) for k in KIND}
    z_in = {k: sb(f"{k}_z", [P, CH], I32) for k in KIND}
    s_in = {k: sb(f"{k}_s", [P, CH]) for k in KIND[:2]}
    w_f = {k: sb(f"{k}_f", [P, CH]) for k in KIND}
    w_h = {k: [sb(f"{k}_h{n}", [P, CH], F32R) for n in range(2)] for k in KIND}
    w_l = {k: [sb(f"{k}_l{n}", [P, CH], F32R) for n in range(2)] for k in KIND}
    one = sb("one", [P, 1])
    dsc = sb("dsc", [P, IT, KT])
    sg = [sb(f"sg{c}", [P, CH]) for c in range(NC)]
    hid = [sb(f"hid{c}", [P, CH]) for c in range(NC)]
    h_h = [sb(f"h_h{n}", [P, TOK], F32R) for n in range(2)]
    h_l = [sb(f"h_l{n}", [P, TOK], F32R) for n in range(2)]
    gate_ps = [stack.enter_context(nc.psum_tensor(f"gate_ps{c}", [P, CH], F32)) for c in range(NC)]
    up_ps = [stack.enter_context(nc.psum_tensor(f"up_ps{c}", [P, CH], F32)) for c in range(NC)]
    y_ps = [stack.enter_context(nc.psum_tensor(f"y_ps{n}", [P, CH], F32)) for n in range(4)]
    UNITS = KT * NC

    ld = {k: sem(f"{k}_ld") for k in KIND}
    w_diff = {k: sem(f"{k}_diff") for k in KIND}
    w_ready = {k: sem(f"{k}_w_ready") for k in KIND}
    w_step, dsc_in, xt_in = sem("w_step"), sem("dsc_in"), sem("xt_in")
    gate_ready, up_ready, sg_ready, hid_ready = sem("gate_ready"), sem("up_ready"), sem("sg_ready"), sem("hid_ready")
    h_hi, h_lo, y_ready, y_added, y_zero = sem("h_hi"), sem("h_lo"), sem("y_ready"), sem("y_added"), sem("y_zero")
    silu_ready, prod_ready, fin_ready, stored = sem("silu_ready"), sem("prod_ready"), sem("fin_ready"), sem("stored")

    block = stack.enter_context(nc.Block())
    LOADS = {"gate": 3, "up": 3, "down": 2}
    STEPS = {"gate": 2, "up": 2, "down": 1}

    @block.sync
    def _(sp):
        def load(k, i, first=False):
            if not first:
                sp.wait_ge(w_ready[k], i)
            sp.dma_start(w_in[k][:, :], mats[k][0][i]).then_inc(ld[k], 16)
            sp.dma_start(z_in[k][:, :], mats[k][1][i].to_broadcast([P, CH])).then_inc(ld[k], 16)
            if k != "down":
                sp.dma_start(s_in[k][:, :], mats[k][2][i].to_broadcast([P, CH])).then_inc(ld[k], 16)

        for k in KIND:
            load(k, 0, first=True)
        sp.dma_start(dsc[:, :, :], down_sc).then_inc(dsc_in, 16)
        sp.dma_start(xt[:, :, :], xT).then_inc(xt_in, 16)
        with sp.Fori(1, IT) as i:
            for k in KIND:
                load(k, i)
        for u in range(UNITS):
            m, c = divmod(u, NC)
            sp.wait_ge(fin_ready, u + 1)
            sp.dma_start(outT[:, m, c * CH:(c + 1) * CH], xt[:, m, c * CH:(c + 1) * CH]).then_inc(stored, 16)
        sp.wait_ge(stored, 16 * UNITS)

    @block.gpsimd
    def _(pool):
        g_ = nc.gpsimd
        g_.memset(yT[:, :, :], 0.0).then_inc(y_zero, 1)
        g_.memset(one[:, :], 1.0).then_inc(y_zero, 1)
        pool.wait_ge(y_zero, 2)

        def weights(k, i, b, wait):
            base = i * 5 + {"gate": 0, "up": 2, "down": 4}[k]
            pool.wait_ge(w_diff[k], i + 1)
            if k != "down":
                g_.tensor_tensor(w_f[k][:, :], w_f[k][:, :], s_in[k][:, :], ALU.mult).then_inc(w_step, 1)
                pool.wait_ge(w_step, base + 1)
            if wait is not None:
                pool.wait_ge(*wait)
            g_.tensor_tensor(w_h[k][b][:, :], w_f[k][:, :], one[:, 0:1].to_broadcast([P, CH]), ALU.mult
                             ).then_inc(w_step, 1)
            pool.wait_ge(w_step, base + STEPS[k])
            g_.tensor_tensor(w_l[k][b][:, :], w_f[k][:, :], f(w_h[k][b][:, :]), ALU.subtract
                             ).then_inc(w_ready[k], 1)

        def hidden_lo(i, c, b):
            cs = slice(c * CH, (c + 1) * CH)
            pool.wait_ge(h_hi, i * NC + (c + 1))
            g_.tensor_tensor(h_l[b][:, cs], hid[c][:, :], f(h_h[b][:, cs]), ALU.subtract).then_inc(h_lo, 1)

        def step(i, b, first=False, last=False):
            if not last:
                weights("gate", i + 1, 1 - b, None if first else (gate_ready, i * NC))
                weights("up", i + 1, 1 - b, None if first else (up_ready, i * NC))
            hidden_lo(i, 0, b)
            hidden_lo(i, 1, b)
            if not last:
                weights("down", i + 1, 1 - b, None if first else (y_ready, i * UNITS))

        weights("gate", 0, 0, None)
        weights("up", 0, 0, None)
        weights("down", 0, 0, None)
        step(0, 0, first=True)
        step(1, 1)
        with pool.Fori(1, IT // 2 - 1) as p:
            step(p * 2, 0)
            step(p * 2 + 1, 1)
        step(IT - 2, 0)
        step(IT - 1, 1, last=True)

    @block.scalar
    def _(act):
        a_ = nc.scalar

        def step(i, b, first=False):
            for c in range(NC):
                cs = slice(c * CH, (c + 1) * CH)
                act.wait_ge(gate_ready, i * NC + (c + 1))
                if not first:
                    act.wait_ge(hid_ready, i * NC + (c - 1))
                a_.activation(sg[c][:, :], gate_ps[c][:, :], ACT.Silu).then_inc(sg_ready, 1)
                act.wait_ge(hid_ready, i * NC + (c + 1))
                if not (first):
                    act.wait_ge(y_ready, (i - 1) * UNITS)
                a_.activation(h_h[b][:, cs], hid[c][:, :], ACT.Copy).then_inc(h_hi, 1)

        step(0, 0, first=True)
        step(1, 1)
        with act.Fori(1, IT // 2) as p:
            step(p * 2, 0)
            step(p * 2 + 1, 1)
        for u in range(UNITS):
            m, c = divmod(u, NC)
            cs = slice(c * CH, (c + 1) * CH)
            act.wait_ge(y_added, UNITS * (IT - 1) + u + 1)
            a_.activation(yT[:, m, cs], yT[:, m, cs], ACT.Silu).then_inc(silu_ready, 1)

    @block.vector
    def _(dve):
        v_ = nc.vector
        dve.wait_ge(y_zero, 2)
        dve.wait_ge(dsc_in, 16)

        def hidden(i, c, first=False):
            dve.wait_ge(sg_ready, i * NC + (c + 1))
            dve.wait_ge(up_ready, i * NC + (c + 1))
            if not first:
                dve.wait_ge(h_lo, i * NC + (c - 1))
            v_.tensor_tensor(hid[c][:, :], sg[c][:, :], up_ps[c][:, :], ALU.mult).then_inc(hid_ready, 1)

        def add(i, units):
            for u in units:
                m, c = divmod(u, NC)
                dst = yT[:, m, c * CH:(c + 1) * CH]
                sc = dsc[:, i, m:m + 1] if isinstance(i, int) else dsc[:, bass.ds(i, 1), m]
                dve.wait_ge(y_ready, i * UNITS + (u + 1))
                if not (isinstance(i, int) and i == 0):
                    dve.wait_ge(y_added, (i - 1) * UNITS + (u + 1))
                v_.scalar_tensor_tensor(out=dst, in0=y_ps[u % 4][:, :], scalar=sc, in1=dst, op0=ALU.mult,
                                        op1=ALU.add).then_inc(y_added, 1)

        def diff(i, kinds):
            for k in kinds:
                dve.wait_ge(ld[k], i * (16 * LOADS[k]) + 16 * LOADS[k])
                if not (isinstance(i, int) and i == 0):
                    dve.wait_ge(w_ready[k], i)
                v_.tensor_tensor(w_f[k][:, :], w_in[k][:, :], z_in[k][:, :], ALU.subtract).then_inc(w_diff[k], 1)

        def step(i, first=False, last=False):
            hidden(i, 0, first)
            if not last:
                diff(i + 1, KIND[:2])
            if not first:
                add(i - 1, range(0, 4))
            hidden(i, 1, first)
            if not first:
                add(i - 1, range(4, 8))
            if not last:
                diff(i + 1, KIND[2:])

        diff(0, KIND)
        step(0, first=True)
        step(1)
        with dve.Fori(1, IT // 2 - 1) as p:
            step(p * 2)
            step(p * 2 + 1)
        step(IT - 2)
        step(IT - 1, last=True)
        add(IT - 1, range(UNITS))
        dve.wait_ge(xt_in, 16)
        for u in range(UNITS):
            m, c = divmod(u, NC)
            cs = slice(c * CH, (c + 1) * CH)
            dve.wait_ge(silu_ready, u + 1)
            v_.tensor_tensor(yT[:, m, cs], yT[:, m, cs], sT[:, m, cs], ALU.mult).then_inc(prod_ready, 1)
            dve.wait_ge(prod_ready, u + 1)
            v_.tensor_tensor(xt[:, m, cs], xt[:, m, cs], yT[:, m, cs], ALU.add).then_inc(fin_ready, 1)

    @block.tensor
    def _(pe):
        mm = nc.tensor.matmul

        def gate_up(i, c, b, first=False):
            cs = slice(c * CH, (c + 1) * CH)
            for k, ps, ready, free in (("gate", gate_ps, gate_ready, sg_ready), ("up", up_ps, up_ready, hid_ready)):
                pe.wait_ge(w_ready[k], i + 1)
                if not first:
                    pe.wait_ge(free, i * NC + (c - 1))
                n = 0
                for kt in range(KT):
                    ws = slice(kt * P, (kt + 1) * P)
                    for a, x_ in ((w_h, xh), (w_h, xl), (w_l, xh)):
                        ins = mm(ps[c][:, :], a[k][b][:, ws], x_[:, kt, cs], start=(n == 0), stop=(n == 3 * KT - 1))
                        n += 1
                ins.then_inc(ready, 1)

        def y_units(i, b, units, first=False):
            pe.wait_ge(h_lo, i * NC + NC)
            pe.wait_ge(w_ready["down"], i + 1)
            for u in units:
                m, c = divmod(u, NC)
                ms_, cs = slice(m * P, (m + 1) * P), slice(c * CH, (c + 1) * CH)
                if not (first and u < 4):
                    pe.wait_ge(y_added, i * UNITS + (u - 3))
                out = y_ps[u % 4][:, :]
                mm(out, w_h["down"][b][:, ms_], h_h[b][:, cs], start=True, stop=False)
                mm(out, w_h["down"][b][:, ms_], h_l[b][:, cs], start=False, stop=False)
                mm(out, w_l["down"][b][:, ms_], h_h[b][:, cs], start=False, stop=True).then_inc(y_ready, 1)

        gate_up(0, 0, 0, first=True)
        gate_up(0, 1, 0, first=True)
        gate_up(1, 0, 1)
        y_units(0, 0, range(0, 4), first=True)
        gate_up(1, 1, 1)
        y_units(0, 0, range(4, 8))
        with pe.Fori(1, IT // 2) as p:
            for b in range(2):
                i = p * 2 + b
                gate_up(i, 0, b)
                y_units(i - 1, 1 - b, range(0, 4))
                gate_up(i, 1, b)
                y_units(i - 1, 1 - b, range(4, 8))
        y_units(IT - 1, 1, range(UNITS))


def program(nc, x, xT, wq, wkv, wo, slopes, qkw, gate, up, down, down_sc, outT):
    with ExitStack() as keep_stack:
        keep = {
            "xh": keep_stack.enter_context(nc.sbuf_tensor("xh", [P, KT, TOK], F32R)),
            "xl": keep_stack.enter_context(nc.sbuf_tensor("xl", [P, KT, TOK], F32R)),
            "s": keep_stack.enter_context(nc.sbuf_tensor("s_acc", [P, KT * TOK], F32)),
        }
        with ExitStack() as stack:
            attention(nc, stack, keep, x, wq, wkv, wo, slopes, qkw)
        with ExitStack() as stack:
            ffn(nc, stack, keep, xT, {"gate": gate, "up": up, "down": down}, down_sc, outT)


def alibi_slopes():
    start = 2 ** (-2 ** (-(np.log2(HEADS) - 3)))
    return np.array([start * start ** i for i in range(HEADS)], dtype=np.float32)


def kernel(**inputs):
    import concourse.bacc as bacc
    from concourse.bass_utils import run_bass_kernel_spmd

    a = {n: np.asarray(v) for n, v in inputs.items()}
    put = np.ascontiguousarray
    x = a["L0_attn_x"].reshape(TOK, DM)
    arrays = {
        "x": put(x.reshape(QT, P, DM)),
        "xT": put(x.T.reshape(KT, P, TOK).transpose(1, 0, 2)),
        "wq": put(a["L0_attn_Wq"].reshape(HEADS, HD, KT, P).transpose(0, 3, 2, 1)),
        "wkv": put(np.concatenate([a[n].reshape(GROUPS, HD, KT, P).transpose(0, 3, 2, 1)
                                   for n in ("L0_attn_Wk", "L0_attn_Wv")], axis=3)),
        "wo": put(a["L0_attn_Wo"].reshape(DM, HEADS, HD).transpose(1, 2, 0)),
        "slopes": put(np.broadcast_to(alibi_slopes(), (P, HEADS))),
        "qkw": put(np.stack([a["L0_attn_q_norm_w"], a["L0_attn_k_norm_w"]], axis=1)),
        "gate_w": put(a["L0_ffn_gate_w"].reshape(KT, P, IT, P).transpose(2, 1, 0, 3)).reshape(IT, P, CH),
        "gate_z": put(a["L0_ffn_gate_z"].reshape(KT, IT, P).transpose(1, 0, 2)).reshape(IT, 1, CH),
        "gate_s": put(a["L0_ffn_gate_s"].reshape(KT, IT, P).transpose(1, 0, 2)).reshape(IT, 1, CH),
        "up_w": put(a["L0_ffn_up_w"].reshape(KT, P, IT, P).transpose(2, 1, 0, 3)).reshape(IT, P, CH),
        "up_z": put(a["L0_ffn_up_z"].reshape(KT, IT, P).transpose(1, 0, 2)).reshape(IT, 1, CH),
        "up_s": put(a["L0_ffn_up_s"].reshape(KT, IT, P).transpose(1, 0, 2)).reshape(IT, 1, CH),
        "down_w": put(a["L0_ffn_down_w"].reshape(IT, P, DM)),
        "down_z": put(a["L0_ffn_down_z"].reshape(IT, 1, DM)),
        "down_s": put(a["L0_ffn_down_s"].reshape(IT, KT, P).transpose(2, 0, 1)),
    }
    nc = bacc.Bacc("TRN2", target_bir_lowering=False, num_devices=1, dynamic_dma_scratch_size=1024)
    d = {n: nc.dram_tensor(f"in_{n}", v.shape, mybir.dt.from_np(v.dtype), kind="ExternalInput").ap()
         for n, v in arrays.items()}
    outT = nc.dram_tensor("outT", (P, KT, TOK), F32, kind="ExternalOutput").ap()
    program(nc, d["x"], d["xT"], d["wq"], d["wkv"], d["wo"], d["slopes"], d["qkw"],
            (d["gate_w"], d["gate_z"], d["gate_s"]), (d["up_w"], d["up_z"], d["up_s"]),
            (d["down_w"], d["down_z"]), d["down_s"], outT)
    r = run_bass_kernel_spmd(nc, [{f"in_{n}": v for n, v in arrays.items()}], core_ids=[0])
    got = r.results[0]["outT"]
    return put(got.transpose(1, 0, 2).reshape(DM, TOK).T).reshape(1, TOK, DM)
```

```python
from contextlib import ExitStack

import numpy as np

import concourse.bass as bass
from concourse import mybir

F32 = mybir.dt.float32
F32R = mybir.dt.float32r
I32 = mybir.dt.int32
ALU = mybir.AluOpType
ACT = mybir.ActivationFunctionType

P = 128
TOK, DM = 1024, 512
HEADS, GROUPS, HD = 32, 8, 128
PER = HEADS // GROUPS
HID = 1792
QT = TOK // P
KT = DM // P
IT = HID // P
CH = 512
NC = TOK // CH
CT = CH // P
LN_EPS, RMS_EPS = 1e-5, 1e-6
MASKED = -1e30

TILES = list(range(QT - 1, -1, -1))
BASE = [P if t == 4 else 0 for t in range(QT)]
CUTS = [[(0, 256)], [(0, 256)], [(0, 384)], [(0, 512)], [(0, 384), (384, 256)], [(0, 512), (512, 256)],
        [(0, 512), (512, 384)], [(0, 512), (512, 512)]]
PBUF = [(0, 1024), (1024, 896), (1920, 768), (2688, 640)]
PBUF_COLS = 3328

STEP = 384
DIAG = [2048 + 1664, 2048]
PT_COLS = 2048 + 1664 + 4 * STEP + STEP


def pt_range(c, kt):
    r = kt - CT * c
    if r < 0:
        return kt * CH, CH, 0
    q0 = min(r, 2) * P
    return DIAG[c] + r * STEP + q0, CH - q0, q0


def parts(t):
    return [(0, 4), (4, t - 3)] if t >= CT else [(0, t + 1)]


PARTS = [(t, n) for t in TILES for n in range(len(parts(t)))]
LN_PARTS = QT


def part_no(h, t, n):
    return LN_PARTS + len(PARTS) * h + PARTS.index((t, n))


PRO = ["kv0", "kv1", "kv2", "kv3", "qc1_0", "ssc1_0"]


def group_order(first, last):
    out = []
    for j in range(PER):
        nx = (j + 1) % PER
        more = not (last and j == PER - 1)
        prev, w = not (first and j == 0), not (first and j < 2)
        out += [f"qc0_{j}"] + [f"v0_{j}"] * prev + [f"ssc0_{j}"] + [f"w0_{j}", f"w1_{j}"] * w
        out += [f"qc1_{nx}"] * more + [f"w2_{j}"] * w + [f"kv{j}"] * (not last)
        out += [f"ssc1_{nx}"] * more + [f"v1_{j}"] + [f"w3_{j}"] * w
    return out


FIRST, STEADY, LAST = group_order(True, False), group_order(False, False), group_order(False, True)
EPI = ["v0_0"] + [f"w{n}" for n in range(8)]


def split_by_act(name):
    return name[0] in "vq"


class Places:

    def __init__(self, kind, g=None):
        self.order = {"pro": PRO, "first": FIRST, "steady": STEADY, "last": LAST, "epi": EPI}[kind]
        hi = lambda names: sum(map(split_by_act, names))
        a, b = len(PRO), hi(PRO)
        if kind == "pro":
            self.a, self.b, self.parity = 0, 0, 0
            return
        if kind == "first":
            self.a, self.b, self.parity = a, b, a % 2
            return
        a, b = a + len(FIRST), b + hi(FIRST)
        self.parity = a % 2
        if kind == "epi":
            self.a, self.b = a + len(STEADY) * (GROUPS - 2) + len(LAST), b + hi(STEADY) * (GROUPS - 2) + hi(LAST)
            self.parity = self.a % 2
            return
        n, m = len(STEADY), hi(STEADY)
        self.a, self.b = g * n + (a - n), g * m + (b - m)

    def n(self, name, more=1):
        return self.a + (self.order.index(name) + more)

    def hi(self, name):
        i = self.order.index(name)
        return self.b + sum(map(split_by_act, self.order[:i + 1]))

    def bank(self, name):
        return (self.parity + self.order.index(name)) % 2


assert len(STEADY) % 2 == 0


def f(ap):
    return ap.bitcast(F32)


def attention(nc, stack, keep, x, wq, wkv, wo, slopes, qkw):
    sb = lambda n, shape, dt=F32: stack.enter_context(nc.sbuf_tensor(n, shape, dt))
    sem = lambda n: stack.enter_context(nc.semaphore(n))
    xh, xl, s_acc = keep["xh"], keep["xl"], keep["s"]
    xs = s_acc[:, :].rearrange("p (i n) -> p i n", i=QT)
    sT = s_acc[:, :].rearrange("p (m n) -> p m n", m=KT)

    pt_h, pt_l = sb("pt_h", [P, PT_COLS], F32R), sb("pt_l", [P, PT_COLS], F32R)
    oT_h, oT_l = sb("oT_h", [P, PER, TOK], F32R), sb("oT_l", [P, PER, TOK], F32R)
    kT_h, kT_l = sb("kT_h", [P, TOK], F32R), sb("kT_l", [P, TOK], F32R)
    v_h, v_l = sb("v_h", [P, QT, HD], F32R), sb("v_l", [P, QT, HD], F32R)
    q_h, q_l = sb("q_h", [P, TOK], F32R), sb("q_l", [P, TOK], F32R)
    wq_h, wq_l = sb("wq_h", [P, KT, HD], F32R), sb("wq_l", [P, KT, HD], F32R)
    wkv_h, wkv_l = sb("wkv_h", [P, KT, 2 * HD], F32R), sb("wkv_l", [P, KT, 2 * HD], F32R)
    wo_h, wo_l = sb("wo_h", [P, PER, DM], F32R), sb("wo_l", [P, PER, DM], F32R)
    wq_in, wkv_in, wo_in = sb("wq_in", [P, KT, HD]), sb("wkv_in", [P, KT, 2 * HD]), sb("wo_in", [P, DM])
    kv = sb("kv", [P, QT, 2 * HD])
    sq = sb("sq", [P, TOK])
    pb = sb("pb", [P, PBUF_COLS])
    rel = sb("rel", [P, TOK])
    junk = sb("junk", [P, HD])
    ident = sb("ident", [P, P])
    ones = sb("ones", [P, QT])
    sl = sb("sl", [P, HEADS])
    qk_w = sb("qk_w", [P, 2])
    qk = sb("qk", [P, 1])
    cst = sb("cst", [P, 3])
    stats = sb("stats", [P, QT, 6])
    mv = sb("mv", [P, QT, 2])
    var_e = sb("var_e", [P, QT])
    rstd = sb("rstd", [P, QT])
    kss, kms, kinv = sb("kss", [P, QT]), sb("kms", [P, QT]), sb("kinv", [P, QT])
    ms, root, inv, ninv, coef = (sb(n, [P, QT]) for n in ("ms", "root", "inv", "ninv", "coef"))
    low, rsum, rinv = sb("low", [P, QT]), sb("rsum", [P, QT]), sb("rinv", [P, QT])

    S = [stack.enter_context(nc.psum_tensor(f"S{n}", [P, 2 * CH], F32)) for n in range(2)]
    T = [stack.enter_context(nc.psum_tensor(f"T{n}", [P, CH], F32)) for n in range(2)]
    O = [stack.enter_context(nc.psum_tensor(f"O{n}", [P, CH], F32)) for n in range(2)]

    LN_BANKS = [T[0][:, :], T[1][:, :]] + [S[n // 2][:, n % 2 * CH:(n % 2 + 1) * CH] for n in range(4)]

    x_in = [sem(f"x_in{i}") for i in range(QT)]
    tab_in = sem("tab_in")
    wq_ld, wkv_ld, wo_ld = sem("wq_ld"), sem("wkv_ld"), sem("wo_ld")
    wq_split, wkv_split, wo_split = sem("wq_split"), sem("wkv_split"), sem("wo_split")
    setup, ln_st, ln_mv, ln_var, ln_rstd, xn_ready = (
        sem("setup"), sem("ln_st"), sem("ln_mv"), sem("ln_var"), sem("ln_rstd"), sem("xn_ready"))
    sT_zero, qk_ready = sem("sT_zero"), sem("qk_ready")
    tr_ready, tr_hi, tr_lo = sem("tr_ready"), sem("tr_hi"), sem("tr_lo")
    out_ready, out_hi, out_free = sem("out_ready"), sem("out_hi"), sem("out_free")
    kss_ready, kms_ready, kinv_ready, kn_ready, v_ready = (
        sem("kss_ready"), sem("kms_ready"), sem("kinv_ready"), sem("kn_ready"), sem("v_ready"))
    kt_ready, kt_hi, kt_lo = sem("kt_ready"), sem("kt_hi"), sem("kt_lo")
    root_ready, coef_ready = sem("root_ready"), sem("coef_ready")
    bias_ready, scores_ready, logits_ready = sem("bias_ready"), sem("scores_ready"), sem("logits_ready")
    exps_ready, rinv_ready, probs_ready = sem("exps_ready"), sem("rinv_ready"), sem("probs_ready")
    wq_hi, wkv_hi, wo_hi, v_hi_done = sem("wq_hi"), sem("wkv_hi"), sem("wo_hi"), sem("v_hi_done")
    SETUP = 7

    def pbuf(idx, t):
        a, w = PBUF[idx % 4]
        return pb[:, a:a + (t + 1) * P]

    def pt_lot(pt, t, n):
        k0, m = parts(t)[n]
        c, ql = t // CT, t % CT
        if k0 == 0 and c == 1:
            return pt[:, 0:4 * CH].rearrange("p (k w) -> p k w", w=CH)[:, :, ql * P:(ql + 1) * P]
        a = DIAG[c] + ql * P
        return pt[:, a:a + m * STEP].rearrange("p (k w) -> p k w", w=STEP)[:, :, 0:P]

    block = stack.enter_context(nc.Block())

    @block.sync
    def _(sp):
        for i in range(QT):
            sp.dma_start(xs[:, i, :], x[i]).then_inc(x_in[i], 16)
            if i == CT - 1:
                sp.dma_start(wkv_in[:, :, :], wkv[0]).then_inc(wkv_ld, 16)
        sp.dma_start(wq_in[:, :, :], wq[0]).then_inc(wq_ld, 16)
        sp.dma_start(sl[:, :], slopes).then_inc(tab_in, 16)
        sp.dma_start(qk_w[:, :], qkw).then_inc(tab_in, 16)
        sp.dma_start(wo_in[:, :], wo[0]).then_inc(wo_ld, 16)


        def group(g, last=False):
            for j in range(PER):
                h = g * PER + j
                if j == 0 and not last:
                    sp.wait_ge(wkv_split, g + 1)
                    sp.dma_start(wkv_in[:, :, :], wkv[g + 1]).then_inc(wkv_ld, 16)
                if not (last and j == PER - 1):
                    sp.wait_ge(wq_split, h + 1)
                    sp.dma_start(wq_in[:, :, :], wq[h + 1]).then_inc(wq_ld, 16)
                    sp.wait_ge(wo_split, h + 1)
                    sp.dma_start(wo_in[:, :], wo[h + 1]).then_inc(wo_ld, 16)

        group(0)
        with sp.Fori(1, GROUPS - 1) as g:
            group(g)
        group(GROUPS - 1, last=True)

    @block.gpsimd
    def _(pool):
        g_ = nc.gpsimd
        g_.memset(ones[:, :], 1.0).then_inc(setup, 1)
        g_.memset(cst[:, 0:1], -0.5).then_inc(setup, 1)
        g_.memset(cst[:, 1:2], 0.5).then_inc(setup, 1)
        g_.memset(cst[:, 2:3], -1.0).then_inc(setup, 1)
        g_.memset(ident[:, :], 0.0).then_inc(setup, 1)
        g_.iota(rel[:, :], pattern=[[1, TOK]], base=-(TOK - P), channel_multiplier=-1,
                allow_small_or_imprecise_dtypes=True).then_inc(setup, 1)
        pool.wait_ge(setup, 6)
        g_.affine_select(out=ident[:, :], in_=ident[:, :], compare_op=ALU.not_equal, fill=1.0, base=0,
                         pattern=[[-1, P]], channel_multiplier=1).then_inc(setup, 1)
        g_.affine_select(out=rel[:, :], in_=rel[:, :], compare_op=ALU.is_ge, fill=MASKED, base=TOK - P,
                         pattern=[[-1, TOK]], channel_multiplier=1).then_inc(setup, 1)
        for c in range(NC):
            a, _, _ = pt_range(c, CT * c + 3)
            for pt in (pt_h, pt_l):
                g_.memset(f(pt[:, a:a + P]), 0.0).then_inc(setup, 1)

        def lo_part(lo, src, hi, hi_done, done, n):
            pool.wait_ge(hi_done, n + 1)
            g_.tensor_tensor(lo, src, f(hi), ALU.subtract).then_inc(done, 1)

        def wq_lo(h):
            lo_part(wq_l[:, :, :], wq_in[:, :, :], wq_h[:, :, :], wq_hi, wq_split, h)

        def wkv_lo(g):
            lo_part(wkv_l[:, :, :], wkv_in[:, :, :], wkv_h[:, :, :], wkv_hi, wkv_split, g)

        def wo_lo(h, j):
            lo_part(wo_l[:, j, :], wo_in[:, :], wo_h[:, j, :], wo_hi, wo_split, h)

        def norms(h, c, value):
            cs = slice(c * CT, (c + 1) * CT)
            n = h * 2 + (1 - c)
            pool.wait_ge(out_free, value)
            half = lambda k: cst[:, k:k + 1].to_broadcast([P, CT])
            g_.tensor_tensor(root[:, cs], ms[:, cs], half(1), ALU.pow).then_inc(root_ready, 1)
            g_.tensor_tensor(inv[:, cs], ms[:, cs], half(0), ALU.pow).then_inc(root_ready, 1)
            pool.wait_ge(root_ready, n * 2 + 2)
            g_.tensor_tensor(ninv[:, cs], inv[:, cs], half(2), ALU.mult).then_inc(coef_ready, 1)
            slope = sl[:, bass.ds(h, 1)] if not isinstance(h, int) else sl[:, h:h + 1]
            g_.tensor_tensor(coef[:, cs], root[:, cs], slope.to_broadcast([P, CT]),
                             ALU.mult).then_inc(coef_ready, 1)

        def bias(h, idx):
            t = TILES[idx]
            c = t // CT
            pool.wait_ge(coef_ready, h * 4 + (2 - c) * 2)
            if idx < 4:
                if not (isinstance(h, int) and h == 0):
                    prev = TILES[idx + 4]
                    pool.wait_ge(tr_ready, part_no(h - 1, prev, len(parts(prev)) - 1) + 1)
            else:
                prev = TILES[idx - 4]
                pool.wait_ge(tr_ready, part_no(h, prev, len(parts(prev)) - 1) + 1)
            w = (t + 1) * P
            g_.tensor_tensor(pbuf(idx, t), rel[:, TOK - w:TOK], coef[:, t:t + 1].to_broadcast([P, w]),
                             ALU.mult).then_inc(bias_ready, 1)

        def k_norm(g):
            pool.wait_ge(kms_ready, g + 1)
            g_.tensor_tensor(kinv[:, :], kms[:, :], cst[:, 0:1].to_broadcast([P, QT]),
                             ALU.pow).then_inc(kinv_ready, 1)
            pool.wait_ge(kinv_ready, g + 1)
            g_.tensor_tensor(kv[:, :, 0:HD], kv[:, :, 0:HD],
                             kinv[:, :].rearrange("p (k o) -> p k o", o=1).to_broadcast([P, QT, HD]),
                             ALU.mult).then_inc(kn_ready, 1)

        pool.wait_ge(setup, SETUP + 5)
        for c in range(NC):
            cs = slice(c * CT, (c + 1) * CT)
            pool.wait_ge(ln_var, c + 1)
            g_.tensor_tensor(rstd[:, cs], var_e[:, cs], cst[:, 0:1].to_broadcast([P, CT]), ALU.pow).then_inc(ln_rstd, 1)
            if c == 0:
                wkv_lo(0)
        wq_lo(0)
        pool.wait_ge(tr_ready, LN_PARTS)
        g_.memset(s_acc[:, :], 0.0).then_inc(sT_zero, 1)
        pool.wait_ge(tab_in, 32)
        k_norm(0)
        norms(0, 1, Places("pro").n("ssc1_0"))
        bias(0, 0)
        bias(0, 1)

        def group(g, kind):
            at = Places(kind, g)
            last = kind == "last"
            for j in range(PER):
                h = g * PER + j
                more = not (last and j == PER - 1)
                bias(h, 2)
                bias(h, 3)
                if j == 0 and not last:
                    wkv_lo(g + 1)
                wo_lo(h, j)
                if more:
                    wq_lo(h + 1)
                norms(h, 0, at.n(f"ssc0_{j}"))
                if j == 0:
                    lo_part(v_l[:, :, :], kv[:, :, HD:2 * HD], v_h[:, :, :], v_hi_done, v_ready, g)
                bias(h, 4)
                bias(h, 5)
                bias(h, 6)
                if more:
                    norms(h + 1, 1, at.n(f"ssc1_{(j + 1) % PER}"))
                bias(h, 7)
                if j == PER - 1 and not last:
                    k_norm(g + 1)
                if more:
                    bias(h + 1, 0)
                    bias(h + 1, 1)

        group(0, "first")
        with pool.Fori(1, GROUPS - 1) as g:
            group(g, "steady")
        group(GROUPS - 1, "last")

    @block.scalar
    def _(act):
        a_ = nc.scalar

        def lot(h, t, n):
            no = part_no(h, t, n)
            m = parts(t)[n][1]
            act.wait_ge(tr_ready, no + 1)
            bank = T[PARTS.index((t, n)) % 2]
            a_.activation(pt_lot(pt_h, t, n), bank[:, 0:m * P].rearrange("p (k w) -> p k w", w=P),
                          ACT.Copy).then_inc(tr_hi, 1)

        def lots(h, t):
            for n in range(len(parts(t))):
                lot(h, t, n)

        def exp(h, idx):
            t = TILES[idx]
            act.wait_ge(logits_ready, h * QT + (idx + 1))
            a_.activation(pbuf(idx, t), pbuf(idx, t), ACT.Exp, bias=low[:, idx:idx + 1], scale=-1.0,
                          accum_out=rsum[:, idx:idx + 1]).then_inc(exps_ready, 1)

        def q_hi(at, name):
            cs = slice(CH * (name[2] == "1"), CH * (name[2] == "1") + CH)
            act.wait_ge(out_ready, at.n(name))
            a_.activation(q_h[:, cs], O[at.bank(name)][:, :], ACT.Copy)
            a_.activation(sq[:, cs], O[at.bank(name)][:, :], ACT.Square).then_inc(out_hi, 1)

        def v_hi(at, name, j):
            cs = slice(CH * (name[1] == "1"), CH * (name[1] == "1") + CH)
            act.wait_ge(out_ready, at.n(name))
            a_.activation(oT_h[:, j, cs], O[at.bank(name)][:, :], ACT.Copy).then_inc(out_hi, 1)

        def k_squares(at, names, g):
            for name in names:
                act.wait_ge(out_free, at.n(name))
                for k in (2 * int(name[2]), 2 * int(name[2]) + 1):
                    if not (isinstance(g, int) and g * QT + k == 0):
                        act.wait_ge(kss_ready, g * QT + k)
                    a_.activation(junk[:, :], kv[:, k, 0:HD], ACT.Square,
                                  accum_out=kss[:, k:k + 1]).then_inc(kss_ready, 1)

        def wq_hi_part(h):
            act.wait_ge(wq_ld, h * 16 + 16)
            a_.activation(wq_h[:, :, :], wq_in[:, :, :], ACT.Copy).then_inc(wq_hi, 1)

        def wkv_hi_part(g):
            act.wait_ge(wkv_ld, g * 16 + 16)
            a_.activation(wkv_h[:, :, :], wkv_in[:, :, :], ACT.Copy).then_inc(wkv_hi, 1)

        def wo_hi_part(h, j):
            act.wait_ge(wo_ld, h * 16 + 16)
            a_.activation(wo_h[:, j, :], wo_in[:, :], ACT.Copy).then_inc(wo_hi, 1)

        wkv_hi_part(0)
        wq_hi_part(0)
        for i in range(QT):
            act.wait_ge(tr_ready, i + 1)
            a_.activation(xh[:, :, i * P:(i + 1) * P], LN_BANKS[i % 6].rearrange("p (k w) -> p k w", w=P),
                          ACT.Copy).then_inc(tr_hi, 1)
        pro = Places("pro")
        k_squares(pro, ["kv0", "kv1", "kv2", "kv3"], 0)
        q_hi(pro, "qc1_0")

        def group(g, kind):
            at = Places(kind, g)
            act.wait_ge(qk_ready, 1)
            act.wait_ge(kt_ready, g + 1)
            a_.activation(kT_h[:, :], S[0][:, :], ACT.Copy, scale=qk[:, 0:1]).then_inc(kt_hi, 1)
            for j in range(PER):
                h = g * PER + j
                more = not (kind == "last" and j == PER - 1)
                prev = not (kind == "first" and j == 0)
                if prev:
                    lots(h - 1, 1)
                    lots(h - 1, 0)
                if j > 0:
                    exp(h, 0)
                elif kind != "last":
                    wkv_hi_part(g + 1)
                q_hi(at, f"qc0_{j}")
                if j == 0:
                    exp(h, 0)
                exp(h, 1)
                if prev:
                    v_hi(at, f"v0_{j}", (j - 1) % PER)
                if j == 0:
                    a_.activation(v_h[:, :, :], kv[:, :, HD:2 * HD], ACT.Copy).then_inc(v_hi_done, 1)
                lots(h, 7)
                wo_hi_part(h, j)
                if more:
                    wq_hi_part(h + 1)
                exp(h, 2)
                lots(h, 6)
                lot(h, 5, 0)
                exp(h, 3)
                lot(h, 5, 1)
                if more:
                    q_hi(at, f"qc1_{(j + 1) % PER}")
                lot(h, 4, 0)
                exp(h, 4)
                lot(h, 4, 1)
                exp(h, 5)
                exp(h, 6)
                lots(h, 3)
                if kind != "last":
                    k_squares(at, [f"kv{j}"], g + 1)
                lots(h, 2)
                v_hi(at, f"v1_{j}", j)
                exp(h, 7)

        group(0, "first")
        with act.Fori(1, GROUPS - 1) as g:
            group(g, "steady")
        group(GROUPS - 1, "last")
        lots(HEADS - 1, 1)
        lots(HEADS - 1, 0)
        v_hi(Places("epi"), "v0_0", PER - 1)

    @block.vector
    def _(dve):
        v_ = nc.vector
        def ln_stats(tiles):
            for i in tiles:
                dve.wait_ge(x_in[i], 16)
                v_.bn_stats(stats[:, i, :], xs[:, i, :]).then_inc(ln_st, 1)

        def ln_variance(c):
            tiles = range(c * CT, (c + 1) * CT)
            for i in tiles:
                dve.wait_ge(ln_st, i + 1)
                v_.bn_aggr(mv[:, i, :], stats[:, i, :]).then_inc(ln_mv, 1)
            dve.wait_ge(ln_mv, (c + 1) * CT)
            cs = slice(c * CT, (c + 1) * CT)
            v_.tensor_scalar(var_e[:, cs], mv[:, cs, 1], LN_EPS, None, ALU.add).then_inc(ln_var, 1)

        def ln_normalise(tiles):
            for i in tiles:
                dve.wait_ge(ln_rstd, i // CT + 1)
                v_.tensor_scalar(xs[:, i, :], xs[:, i, :], mv[:, i, 0:1], rstd[:, i:i + 1], ALU.subtract,
                                 ALU.mult).then_inc(xn_ready, 1)

        def ln_lo(tiles):
            for i in tiles:
                dve.wait_ge(tr_hi, i + 1)
                cs = slice(i * P, (i + 1) * P)
                v_.tensor_tensor(xl[:, :, cs], LN_BANKS[i % 6].rearrange("p (k w) -> p k w", w=P),
                                 f(xh[:, :, cs]), ALU.subtract).then_inc(tr_lo, 1)

        ln_stats(range(0, 4))
        ln_variance(0)
        ln_stats(range(4, 6))
        ln_normalise(range(0, 4))
        ln_stats(range(6, 8))
        ln_variance(1)
        ln_lo(range(0, 2))
        ln_normalise(range(4, 6))
        ln_lo(range(2, 4))
        ln_normalise(range(6, 8))
        ln_lo(range(4, 6))

        def lot(h, t, n):
            m = parts(t)[n][1]
            dve.wait_ge(tr_hi, part_no(h, t, n) + 1)
            bank = T[PARTS.index((t, n)) % 2]
            v_.tensor_tensor(pt_lot(pt_l, t, n), bank[:, 0:m * P].rearrange("p (k w) -> p k w", w=P),
                             f(pt_lot(pt_h, t, n)), ALU.subtract).then_inc(tr_lo, 1)

        def lots(h, t):
            for n in range(len(parts(t))):
                lot(h, t, n)

        def logits(h, idx):
            t = TILES[idx]
            n = h * QT + (idx + 1)
            dve.compute_val(n)
            dve.wait_ge(setup, SETUP + 5)
            dve.wait_ge(bias_ready, n)
            dve.wait_ge(scores_ready, n)
            v_.tensor_tensor_reduce(out=pbuf(idx, t), in0=S[idx % 2][:, BASE[t]:BASE[t] + (t + 1) * P],
                                    in1=pbuf(idx, t), scale=ninv[:, t:t + 1], scalar=3e38, op0=ALU.add,
                                    op1=ALU.min, accum_out=low[:, idx:idx + 1]).then_inc(logits_ready, 1)

        def normalise(h, idx):
            dve.wait_ge(exps_ready, h * QT + (idx + 1))
            v_.reciprocal(rinv[:, idx:idx + 1], rsum[:, idx:idx + 1]).then_inc(rinv_ready, 1)
            t = TILES[idx]
            dve.wait_ge(rinv_ready, h * QT + (idx + 1))
            v_.tensor_scalar(pbuf(idx, t), pbuf(idx, t), rinv[:, idx:idx + 1], None, ALU.mult
                             ).then_inc(probs_ready, 1)

        def q_lo(at, name):
            cs = slice(CH * (name[2] == "1"), CH * (name[2] == "1") + CH)
            dve.wait_ge(out_hi, at.hi(name))
            v_.tensor_tensor(q_l[:, cs], O[at.bank(name)][:, :], f(q_h[:, cs]), ALU.subtract).then_inc(out_free, 1)

        def v_lo(at, name, j):
            cs = slice(CH * (name[1] == "1"), CH * (name[1] == "1") + CH)
            dve.wait_ge(out_hi, at.hi(name))
            v_.tensor_tensor(oT_l[:, j, cs], O[at.bank(name)][:, :], f(oT_h[:, j, cs]),
                             ALU.subtract).then_inc(out_free, 1)

        def mean_sq(at, name):
            cs = slice(CT * (name[3] == "1"), CT * (name[3] == "1") + CT)
            dve.wait_ge(out_ready, at.n(name))
            v_.tensor_scalar(ms[:, cs], O[at.bank(name)][:, 0:CT], HD * RMS_EPS, None,
                             ALU.add).then_inc(out_free, 1)

        def kv_copy(at, names, g):
            for name in names:
                k = 2 * int(name[2])
                dve.wait_ge(v_ready, g)
                dve.wait_ge(out_ready, at.n(name))
                v_.tensor_copy(kv[:, k:k + 2, :], O[at.bank(name)][:, :].rearrange("p (k w) -> p k w", w=2 * HD)
                               ).then_inc(out_free, 1)

        def k_mean_sq(g):
            dve.wait_ge(kss_ready, g * QT + QT)
            v_.tensor_scalar(kms[:, :], kss[:, :], 1.0 / HD, RMS_EPS, ALU.mult, ALU.add).then_inc(kms_ready, 1)

        def project(at, name, unit):
            m, c = divmod(unit, NC)
            dst = sT[:, m, c * CH:(c + 1) * CH]
            dve.wait_ge(out_ready, at.n(name))
            v_.tensor_tensor(dst, O[at.bank(name)][:, :], dst, ALU.add).then_inc(out_free, 1)

        pro = Places("pro")
        for n in range(4):
            if n == 1:
                ln_lo(range(6, 8))
                dve.wait_ge(tab_in, 32)
                v_.tensor_tensor(qk[:, :], qk_w[:, 0:1], qk_w[:, 1:2], ALU.mult).then_inc(qk_ready, 1)
            dve.wait_ge(out_ready, pro.n(f"kv{n}"))
            v_.tensor_copy(kv[:, 2 * n:2 * n + 2, :], O[pro.bank(f"kv{n}")][:, :].rearrange("p (k w) -> p k w", w=2 * HD)
                           ).then_inc(out_free, 1)
        k_mean_sq(0)
        q_lo(pro, "qc1_0")
        mean_sq(pro, "ssc1_0")
        dve.wait_ge(sT_zero, 1)

        def group(g, kind):
            at = Places(kind, g)
            last = kind == "last"
            if kind != "first":
                normalise(g * PER - 1, 7)
            dve.wait_ge(kt_hi, g + 1)
            v_.scalar_tensor_tensor(out=kT_l[:, :], in0=S[0][:, :], scalar=qk[:, 0:1], in1=f(kT_h[:, :]),
                                    op0=ALU.mult, op1=ALU.subtract).then_inc(kt_lo, 1)
            for j in range(PER):
                h = g * PER + j
                nx = (j + 1) % PER
                more = not (last and j == PER - 1)
                prev = not (kind == "first" and j == 0)
                w = not (kind == "first" and j < 2)
                unit = 4 * (j % 2)
                if prev and j > 0:
                    normalise(h - 1, 7)
                if j > 0:
                    logits(h, 0)
                if prev:
                    lots(h - 1, 1)
                    lots(h - 1, 0)
                if j > 0:
                    normalise(h, 0)
                else:
                    logits(h, 0)
                q_lo(at, f"qc0_{j}")
                logits(h, 1)
                if j == 0:
                    normalise(h, 0)
                normalise(h, 1)
                if prev:
                    v_lo(at, f"v0_{j}", (j - 1) % PER)
                mean_sq(at, f"ssc0_{j}")
                lot(h, 7, 0)
                logits(h, 2)
                lot(h, 7, 1)
                if w:
                    project(at, f"w0_{j}", unit)
                lot(h, 6, 0)
                normalise(h, 2)
                if w:
                    project(at, f"w1_{j}", unit + 1)
                lot(h, 6, 1)
                logits(h, 3)
                lot(h, 5, 0)
                normalise(h, 3)
                lot(h, 5, 1)
                logits(h, 4)
                if more:
                    q_lo(at, f"qc1_{nx}")
                lot(h, 4, 0)
                normalise(h, 4)
                if w:
                    project(at, f"w2_{j}", unit + 2)
                lot(h, 4, 1)
                logits(h, 5)
                normalise(h, 5)
                if not last:
                    kv_copy(at, [f"kv{j}"], g + 1)
                if more:
                    mean_sq(at, f"ssc1_{nx}")
                logits(h, 6)
                lots(h, 3)
                if j == PER - 1 and not last:
                    k_mean_sq(g + 1)
                normalise(h, 6)
                lots(h, 2)
                v_lo(at, f"v1_{j}", j)
                if w:
                    project(at, f"w3_{j}", unit + 3)
                logits(h, 7)

        group(0, "first")
        with dve.Fori(1, GROUPS - 1) as g:
            group(g, "steady")
        group(GROUPS - 1, "last")
        normalise(HEADS - 1, 7)
        lots(HEADS - 1, 1)
        lots(HEADS - 1, 0)
        epi = Places("epi")
        v_lo(epi, "v0_0", PER - 1)
        for n in range(KT * NC):
            project(epi, f"w{n}", n)

    @block.tensor
    def _(pe):
        mm = nc.tensor.matmul

        def products(out, terms, between=None, done=0):
            n = 0
            for ah, al, bh, bl in terms:
                for a, b in ((ah, bh), (ah, bl), (al, bh)):
                    ins = mm(out, a, b, start=(n == 0), stop=(n == 3 * len(terms) - 1))
                    n += 1
                    for work in (between or {}).get(done + n, ()):
                        work()
            return ins

        def take(at, name):
            first2 = at.order is PRO and at.order.index(name) < 2
            if not first2:
                pe.wait_ge(out_free, at.n(name, more=-1))
            return O[at.bank(name)]

        def lot(h, t, n):
            idx = TILES.index(t)
            k0, m = parts(t)[n]
            no = part_no(h, t, n)
            pe.wait_ge(probs_ready, h * QT + (idx + 1))
            pe.wait_ge(tr_lo, no - 1)
            bank = T[PARTS.index((t, n)) % 2]
            for k in range(m):
                ins = nc.tensor.transpose(bank[:, k * P:(k + 1) * P],
                                          pbuf(idx, t)[:, (k0 + k) * P:(k0 + k + 1) * P], ident[:, :])
            ins.then_inc(tr_ready, 1)

        def lots(h, t):
            for n in range(len(parts(t))):
                lot(h, t, n)

        def scores(h, idx):
            t = TILES[idx]
            if not (isinstance(h, int) and h == 0 and idx < 2):
                pe.wait_ge(logits_ready, h * QT + (idx - 1))
            bank = S[idx % 2]
            qs = slice(t * P, (t + 1) * P)
            cuts = CUTS[t]
            for q, last in ((q_h, False), (q_l, True)):
                for k0, w in cuts:
                    out = bank[:, BASE[t] + k0:BASE[t] + k0 + w]
                    if not last:
                        mm(out, q[:, qs], kT_h[:, k0:k0 + w], start=True, stop=False)
                        mm(out, q[:, qs], kT_l[:, k0:k0 + w], start=False, stop=False)
                    else:
                        ins = mm(out, q[:, qs], kT_h[:, k0:k0 + w], start=False, stop=True)
            ins.then_inc(scores_ready, 1)

        def values(at, name, h, wait, between=None):
            c = int(name[1])
            out = take(at, name)
            last_t = c * CT
            pe.wait_ge(tr_lo, part_no(h, last_t, len(parts(last_t)) - 1) + 1)
            if wait is not None:
                pe.wait_ge(v_ready, wait)
            n = CT * (c + 1)
            for kt in range(n):
                a, w, q0 = pt_range(c, kt)
                o = out[:, q0:q0 + w]
                for i, (v, pt) in enumerate(((v_h, pt_h), (v_h, pt_l), (v_l, pt_h))):
                    ins = mm(o, v[:, kt, :], pt[:, a:a + w], start=(kt + i == 0), stop=(kt == n - 1 and i == 2))
                    for work in (between or {}).get(3 * kt + i + 1, ()):
                        work()
            ins.then_inc(out_ready, 1)

        def q_proj(at, name, h, between=None):
            c = int(name[2])
            out = take(at, name)
            pe.wait_ge(wq_split, h + 1)
            cs = slice(c * CH, (c + 1) * CH)
            products(out[:, :], [(wq_h[:, k, :], wq_l[:, k, :], xh[:, k, cs], xl[:, k, cs]) for k in range(KT)],
                     between).then_inc(out_ready, 1)

        def sums(at, name, of, i):
            c = int(name[3])
            if i == 0:
                take(at, name)
                pe.wait_ge(out_hi, at.hi(of))
            a = (c * CT + i) * P
            ins = mm(O[at.bank(name)][:, i:i + 1], sq[:, a:a + P], ones[:, 0:1], start=True, stop=True)
            if i == CT - 1:
                ins.then_inc(out_ready, 1)

        def sums_between(at, name, of, after):
            return {n: [lambda i=i: sums(at, name, of, i)] for i, n in enumerate(after)}

        def kv_proj(at, name, g, between=None):
            out = take(at, name)
            pe.wait_ge(wkv_split, g + 1)
            for i in range(2):
                a = (2 * int(name[2]) + i) * P
                ins = products(out[:, i * 2 * HD:(i + 1) * 2 * HD],
                               [(xh[:, k, a:a + P], xl[:, k, a:a + P], wkv_h[:, k, :], wkv_l[:, k, :])
                                for k in range(KT)], between, i * 3 * KT)
            ins.then_inc(out_ready, 1)

        def k_transposes(g):
            pe.wait_ge(kn_ready, g + 1)
            if not (isinstance(g, int) and g == 0):
                pe.wait_ge(logits_ready, g * (PER * QT) - 1)
            for k in range(QT):
                ins = nc.tensor.transpose(S[0][:, k * P:(k + 1) * P], kv[:, k, 0:HD], ident[:, :])
            ins.then_inc(kt_ready, 1)

        def project(at, name, unit, h0, v0):
            m, c = divmod(unit, NC)
            j0 = 0 if v0 == "v0_2" else 2
            out = take(at, name)
            pe.wait_ge(wo_split, h0 + 2)
            pe.wait_ge(out_free, at.n(v0))
            ms_, cs = slice(m * P, (m + 1) * P), slice(c * CH, (c + 1) * CH)
            products(out[:, :], [(wo_h[:, j, ms_], wo_l[:, j, ms_], oT_h[:, j, cs], oT_l[:, j, cs])
                                 for j in (j0, j0 + 1)]).then_inc(out_ready, 1)

        pe.wait_ge(setup, SETUP + 5)
        pro = Places("pro")

        def ln_transposes(tiles):
            for i in tiles:
                pe.wait_ge(xn_ready, i + 1)
                if i >= 6:
                    pe.wait_ge(tr_lo, i - 5)
                for k in range(KT):
                    ins = nc.tensor.transpose(LN_BANKS[i % 6][:, k * P:(k + 1) * P],
                                              xs[:, i, k * P:(k + 1) * P], ident[:, :])
                ins.then_inc(tr_ready, 1)

        ln_transposes(range(0, 6))
        for n in range(4):
            pe.wait_ge(tr_lo, 2 * n + 2)
            kv_proj(pro, f"kv{n}", 0)
            if n == 0:
                ln_transposes(range(6, 8))
        q_proj(pro, "qc1_0", 0)
        for i in range(CT):
            sums(pro, "ssc1_0", "qc1_0", i)

        def group(g, kind):
            at = Places(kind, g)
            last = kind == "last"
            if kind == "first":
                q_proj(at, "qc0_0", 0)
            k_transposes(g)
            for j in range(PER):
                h = g * PER + j
                nx = (j + 1) % PER
                more = not (last and j == PER - 1)
                prev = not (kind == "first" and j == 0)

                def w_unit(n, h=h, j=j):
                    if kind == "first" and j < 2:
                        return
                    project(at, f"w{n}_{j}", 4 * (j % 2) + n, h - 2 - j % 2, f"v0_{j - j % 2}")

                if j > 0:
                    scores(h, 0)
                if prev:
                    lots(h - 1, 1)
                    q_proj(at, f"qc0_{j}", h, {6: [lambda h=h: lots(h - 1, 0)]})
                elif j > 0:
                    q_proj(at, f"qc0_{j}", h)
                if j == 0:
                    pe.wait_ge(kt_lo, g + 1)
                    scores(h, 0)
                scores(h, 1)
                if prev:
                    values(at, f"v0_{j}", h - 1, None, sums_between(at, f"ssc0_{j}", f"qc0_{j}", (9, 10, 11, 12)))
                else:
                    for i in range(CT):
                        sums(at, f"ssc0_{j}", f"qc0_{j}", i)
                lots(h, 7)
                scores(h, 2)
                w_unit(0)
                lot(h, 6, 0)
                w_unit(1)
                lot(h, 6, 1)
                scores(h, 3)
                lot(h, 5, 0)
                if more:
                    q_proj(at, f"qc1_{nx}", h + 1, {6: [lambda h=h: lot(h, 5, 1)]})
                else:
                    lot(h, 5, 1)
                scores(h, 4)
                lot(h, 4, 0)
                w_unit(2)
                lot(h, 4, 1)
                scores(h, 5)
                if not last:
                    kv_proj(at, f"kv{j}", g + 1, sums_between(at, f"ssc1_{nx}", f"qc1_{nx}", (12, 16, 20, 24)))
                elif more:
                    for i in range(CT):
                        sums(at, f"ssc1_{nx}", f"qc1_{nx}", i)
                scores(h, 6)
                lots(h, 3)
                values(at, f"v1_{j}", h, g + 1 if j == 0 else None, {12: [lambda h=h: lots(h, 2)]})
                w_unit(3)
                scores(h, 7)

        group(0, "first")
        with pe.Fori(1, GROUPS - 1) as g:
            group(g, "steady")
        group(GROUPS - 1, "last")
        lots(HEADS - 1, 1)
        lots(HEADS - 1, 0)
        epi = Places("epi")
        values(epi, "v0_0", HEADS - 1, None)
        for n in range(KT * NC):
            project(epi, f"w{n}", n, HEADS - 2, "v0_0")


def ffn(nc, stack, keep, xT, mats, down_sc, outT):
    sb = lambda n, shape, dt=F32: stack.enter_context(nc.sbuf_tensor(n, shape, dt))
    sem = lambda n: stack.enter_context(nc.semaphore(n))
    xh, xl = keep["xh"], keep["xl"]
    sT = keep["s"][:, :].rearrange("p (m n) -> p m n", m=KT)
    yT = sb("yT", [P, KT, TOK])
    xt = sb("xt", [P, KT, TOK])
    KIND = ("gate", "up", "down")
    w_in = {k: sb(f"{k}_in", [P, CH], I32) for k in KIND}
    z_in = {k: sb(f"{k}_z", [P, CH], I32) for k in KIND}
    s_in = {k: sb(f"{k}_s", [P, CH]) for k in KIND[:2]}
    w_f = {k: sb(f"{k}_f", [P, CH]) for k in KIND}
    w_h = {k: [sb(f"{k}_h{n}", [P, CH], F32R) for n in range(2)] for k in KIND}
    w_l = {k: [sb(f"{k}_l{n}", [P, CH], F32R) for n in range(2)] for k in KIND}
    dsc = sb("dsc", [P, IT, KT])
    sg = [sb(f"sg{c}", [P, CH]) for c in range(NC)]
    hid = [sb(f"hid{c}", [P, CH]) for c in range(NC)]
    h_h = [sb(f"h_h{n}", [P, TOK], F32R) for n in range(2)]
    h_l = [sb(f"h_l{n}", [P, TOK], F32R) for n in range(2)]
    gate_ps = [stack.enter_context(nc.psum_tensor(f"gate_ps{c}", [P, CH], F32)) for c in range(NC)]
    up_ps = [stack.enter_context(nc.psum_tensor(f"up_ps{c}", [P, CH], F32)) for c in range(NC)]
    y_ps = [stack.enter_context(nc.psum_tensor(f"y_ps{n}", [P, CH], F32)) for n in range(4)]
    UNITS = KT * NC

    ld = {k: sem(f"{k}_ld") for k in KIND}
    w_diff = {k: sem(f"{k}_diff") for k in KIND}
    w_ready = {k: sem(f"{k}_w_ready") for k in KIND}
    w_hi = {k: sem(f"{k}_w_hi") for k in KIND}
    w_scaled = {k: sem(f"{k}_scaled") for k in KIND[:2]}
    dsc_in, xt_in = sem("dsc_in"), sem("xt_in")
    gate_ready, up_ready, sg_ready, hid_ready = sem("gate_ready"), sem("up_ready"), sem("sg_ready"), sem("hid_ready")
    h_hi, h_lo, y_ready, y_added, y_zero = sem("h_hi"), sem("h_lo"), sem("y_ready"), sem("y_added"), sem("y_zero")
    silu_ready, prod_ready, fin_ready, stored = sem("silu_ready"), sem("prod_ready"), sem("fin_ready"), sem("stored")

    block = stack.enter_context(nc.Block())
    LOADS = {"gate": 3, "up": 3, "down": 2}

    @block.sync
    def _(sp):
        def load(k, i, first=False):
            if not first:
                sp.wait_ge(w_ready[k], i)
            sp.dma_start(w_in[k][:, :], mats[k][0][i]).then_inc(ld[k], 16)
            sp.dma_start(z_in[k][:, :], mats[k][1][i].to_broadcast([P, CH])).then_inc(ld[k], 16)
            if k != "down":
                sp.dma_start(s_in[k][:, :], mats[k][2][i].to_broadcast([P, CH])).then_inc(ld[k], 16)

        for k in KIND:
            load(k, 0, first=True)
        sp.dma_start(dsc[:, :, :], down_sc).then_inc(dsc_in, 16)
        sp.dma_start(xt[:, :, :], xT).then_inc(xt_in, 16)
        with sp.Fori(1, IT) as i:
            for k in KIND:
                load(k, i)
        for u in range(UNITS):
            m, c = divmod(u, NC)
            sp.wait_ge(fin_ready, u + 1)
            sp.dma_start(outT[:, m, c * CH:(c + 1) * CH], xt[:, m, c * CH:(c + 1) * CH]).then_inc(stored, 16)
        sp.wait_ge(stored, 16 * UNITS)

    @block.gpsimd
    def _(pool):
        g_ = nc.gpsimd
        g_.memset(yT[:, :, :], 0.0).then_inc(y_zero, 1)

        def scale(k, i):
            pool.wait_ge(w_diff[k], i + 1)
            g_.tensor_tensor(w_f[k][:, :], w_f[k][:, :], s_in[k][:, :], ALU.mult).then_inc(w_scaled[k], 1)

        def weights(k, i, b):
            pool.wait_ge(w_hi[k], i + 1)
            g_.tensor_tensor(w_l[k][b][:, :], w_f[k][:, :], f(w_h[k][b][:, :]), ALU.subtract
                             ).then_inc(w_ready[k], 1)

        def hidden_lo(i, c, b):
            cs = slice(c * CH, (c + 1) * CH)
            pool.wait_ge(h_hi, i * NC + (c + 1))
            g_.tensor_tensor(h_l[b][:, cs], hid[c][:, :], f(h_h[b][:, cs]), ALU.subtract).then_inc(h_lo, 1)

        def step(i, b, last=False):
            if not last:
                scale("gate", i + 1)
                scale("up", i + 1)
            hidden_lo(i, 0, b)
            if not last:
                weights("gate", i + 1, 1 - b)
                weights("up", i + 1, 1 - b)
            hidden_lo(i, 1, b)
            if not last:
                weights("down", i + 1, 1 - b)

        scale("gate", 0)
        scale("up", 0)
        for k in KIND:
            weights(k, 0, 0)
        step(0, 0)
        step(1, 1)
        with pool.Fori(1, IT // 2 - 1) as p:
            step(p * 2, 0)
            step(p * 2 + 1, 1)
        step(IT - 2, 0)
        step(IT - 1, 1, last=True)

    @block.scalar
    def _(act):
        a_ = nc.scalar

        def weights(k, i, b, wait=None):
            act.wait_ge(w_diff[k] if k == "down" else w_scaled[k], i + 1)
            if wait is not None:
                act.wait_ge(*wait)
            a_.activation(w_h[k][b][:, :], w_f[k][:, :], ACT.Copy).then_inc(w_hi[k], 1)

        def step(i, b, first=False, last=False):
            for c in range(NC):
                cs = slice(c * CH, (c + 1) * CH)
                act.wait_ge(gate_ready, i * NC + (c + 1))
                if not first:
                    act.wait_ge(hid_ready, i * NC + (c - 1))
                a_.activation(sg[c][:, :], gate_ps[c][:, :], ACT.Silu).then_inc(sg_ready, 1)
                act.wait_ge(hid_ready, i * NC + (c + 1))
                if not (first):
                    act.wait_ge(y_ready, (i - 1) * UNITS)
                a_.activation(h_h[b][:, cs], hid[c][:, :], ACT.Copy).then_inc(h_hi, 1)
                if last:
                    continue
                if c == 0:
                    weights("gate", i + 1, 1 - b, None if first else (gate_ready, i * NC))
                    weights("up", i + 1, 1 - b, None if first else (up_ready, i * NC))
                else:
                    weights("down", i + 1, 1 - b, None if first else (y_ready, i * UNITS))

        for k in KIND:
            weights(k, 0, 0)
        step(0, 0, first=True)
        step(1, 1)
        with act.Fori(1, IT // 2 - 1) as p:
            step(p * 2, 0)
            step(p * 2 + 1, 1)
        step(IT - 2, 0)
        step(IT - 1, 1, last=True)
        for u in range(UNITS):
            m, c = divmod(u, NC)
            cs = slice(c * CH, (c + 1) * CH)
            act.wait_ge(y_added, UNITS * (IT - 1) + u + 1)
            a_.activation(yT[:, m, cs], yT[:, m, cs], ACT.Silu).then_inc(silu_ready, 1)

    @block.vector
    def _(dve):
        v_ = nc.vector
        dve.wait_ge(y_zero, 1)
        dve.wait_ge(dsc_in, 16)

        def hidden(i, c, first=False):
            dve.wait_ge(sg_ready, i * NC + (c + 1))
            dve.wait_ge(up_ready, i * NC + (c + 1))
            if not first:
                dve.wait_ge(h_lo, i * NC + (c - 1))
            v_.tensor_tensor(hid[c][:, :], sg[c][:, :], up_ps[c][:, :], ALU.mult).then_inc(hid_ready, 1)

        def add(i, units):
            for u in units:
                m, c = divmod(u, NC)
                dst = yT[:, m, c * CH:(c + 1) * CH]
                sc = dsc[:, i, m:m + 1] if isinstance(i, int) else dsc[:, bass.ds(i, 1), m]
                dve.wait_ge(y_ready, i * UNITS + (u + 1))
                if not (isinstance(i, int) and i == 0):
                    dve.wait_ge(y_added, (i - 1) * UNITS + (u + 1))
                v_.scalar_tensor_tensor(out=dst, in0=y_ps[u % 4][:, :], scalar=sc, in1=dst, op0=ALU.mult,
                                        op1=ALU.add).then_inc(y_added, 1)

        def diff(i, kinds):
            for k in kinds:
                dve.wait_ge(ld[k], i * (16 * LOADS[k]) + 16 * LOADS[k])
                if not (isinstance(i, int) and i == 0):
                    dve.wait_ge(w_ready[k], i)
                v_.tensor_tensor(w_f[k][:, :], w_in[k][:, :], z_in[k][:, :], ALU.subtract).then_inc(w_diff[k], 1)

        def step(i, first=False, last=False):
            hidden(i, 0, first)
            if not last:
                diff(i + 1, KIND[:2])
            if not first:
                add(i - 1, range(0, 4))
            hidden(i, 1, first)
            if not first:
                add(i - 1, range(4, 8))
            if not last:
                diff(i + 1, KIND[2:])

        diff(0, KIND)
        step(0, first=True)
        step(1)
        with dve.Fori(1, IT // 2 - 1) as p:
            step(p * 2)
            step(p * 2 + 1)
        step(IT - 2)
        step(IT - 1, last=True)
        add(IT - 1, range(UNITS))
        dve.wait_ge(xt_in, 16)
        for u in range(UNITS):
            m, c = divmod(u, NC)
            cs = slice(c * CH, (c + 1) * CH)
            dve.wait_ge(silu_ready, u + 1)
            v_.tensor_tensor(yT[:, m, cs], yT[:, m, cs], sT[:, m, cs], ALU.mult).then_inc(prod_ready, 1)
            dve.wait_ge(prod_ready, u + 1)
            v_.tensor_tensor(xt[:, m, cs], xt[:, m, cs], yT[:, m, cs], ALU.add).then_inc(fin_ready, 1)

    @block.tensor
    def _(pe):
        mm = nc.tensor.matmul

        def gate_up(i, c, b, first=False):
            cs = slice(c * CH, (c + 1) * CH)
            for k, ps, ready, free in (("gate", gate_ps, gate_ready, sg_ready), ("up", up_ps, up_ready, hid_ready)):
                pe.wait_ge(w_ready[k], i + 1)
                if not first:
                    pe.wait_ge(free, i * NC + (c - 1))
                n = 0
                for kt in range(KT):
                    ws = slice(kt * P, (kt + 1) * P)
                    for a, x_ in ((w_h, xh), (w_h, xl), (w_l, xh)):
                        ins = mm(ps[c][:, :], a[k][b][:, ws], x_[:, kt, cs], start=(n == 0), stop=(n == 3 * KT - 1))
                        n += 1
                ins.then_inc(ready, 1)

        def y_units(i, b, units, first=False):
            pe.wait_ge(h_lo, i * NC + NC)
            pe.wait_ge(w_ready["down"], i + 1)
            for u in units:
                m, c = divmod(u, NC)
                ms_, cs = slice(m * P, (m + 1) * P), slice(c * CH, (c + 1) * CH)
                if not (first and u < 4):
                    pe.wait_ge(y_added, i * UNITS + (u - 3))
                out = y_ps[u % 4][:, :]
                mm(out, w_h["down"][b][:, ms_], h_h[b][:, cs], start=True, stop=False)
                mm(out, w_h["down"][b][:, ms_], h_l[b][:, cs], start=False, stop=False)
                mm(out, w_l["down"][b][:, ms_], h_h[b][:, cs], start=False, stop=True).then_inc(y_ready, 1)

        gate_up(0, 0, 0, first=True)
        gate_up(0, 1, 0, first=True)
        gate_up(1, 0, 1)
        y_units(0, 0, range(0, 4), first=True)
        gate_up(1, 1, 1)
        y_units(0, 0, range(4, 8))
        with pe.Fori(1, IT // 2) as p:
            for b in range(2):
                i = p * 2 + b
                gate_up(i, 0, b)
                y_units(i - 1, 1 - b, range(0, 4))
                gate_up(i, 1, b)
                y_units(i - 1, 1 - b, range(4, 8))
        y_units(IT - 1, 1, range(UNITS))


def program(nc, x, xT, wq, wkv, wo, slopes, qkw, gate, up, down, down_sc, outT):
    with ExitStack() as keep_stack:
        keep = {
            "xh": keep_stack.enter_context(nc.sbuf_tensor("xh", [P, KT, TOK], F32R)),
            "xl": keep_stack.enter_context(nc.sbuf_tensor("xl", [P, KT, TOK], F32R)),
            "s": keep_stack.enter_context(nc.sbuf_tensor("s_acc", [P, KT * TOK], F32)),
        }
        with ExitStack() as stack:
            attention(nc, stack, keep, x, wq, wkv, wo, slopes, qkw)
        with ExitStack() as stack:
            ffn(nc, stack, keep, xT, {"gate": gate, "up": up, "down": down}, down_sc, outT)


def alibi_slopes():
    start = 2 ** (-2 ** (-(np.log2(HEADS) - 3)))
    return np.array([start * start ** i for i in range(HEADS)], dtype=np.float32)


def kernel(**inputs):
    import concourse.bacc as bacc
    from concourse.bass_utils import run_bass_kernel_spmd

    a = {n: np.asarray(v) for n, v in inputs.items()}
    put = np.ascontiguousarray
    x = a["L0_attn_x"].reshape(TOK, DM)
    arrays = {
        "x": put(x.reshape(QT, P, DM)),
        "xT": put(x.T.reshape(KT, P, TOK).transpose(1, 0, 2)),
        "wq": put(a["L0_attn_Wq"].reshape(HEADS, HD, KT, P).transpose(0, 3, 2, 1)),
        "wkv": put(np.concatenate([a[n].reshape(GROUPS, HD, KT, P).transpose(0, 3, 2, 1)
                                   for n in ("L0_attn_Wk", "L0_attn_Wv")], axis=3)),
        "wo": put(a["L0_attn_Wo"].reshape(DM, HEADS, HD).transpose(1, 2, 0)),
        "slopes": put(np.broadcast_to(alibi_slopes(), (P, HEADS))),
        "qkw": put(np.stack([a["L0_attn_q_norm_w"], a["L0_attn_k_norm_w"]], axis=1)),
        "gate_w": put(a["L0_ffn_gate_w"].reshape(KT, P, IT, P).transpose(2, 1, 0, 3)).reshape(IT, P, CH),
        "gate_z": put(a["L0_ffn_gate_z"].reshape(KT, IT, P).transpose(1, 0, 2)).reshape(IT, 1, CH),
        "gate_s": put(a["L0_ffn_gate_s"].reshape(KT, IT, P).transpose(1, 0, 2)).reshape(IT, 1, CH),
        "up_w": put(a["L0_ffn_up_w"].reshape(KT, P, IT, P).transpose(2, 1, 0, 3)).reshape(IT, P, CH),
        "up_z": put(a["L0_ffn_up_z"].reshape(KT, IT, P).transpose(1, 0, 2)).reshape(IT, 1, CH),
        "up_s": put(a["L0_ffn_up_s"].reshape(KT, IT, P).transpose(1, 0, 2)).reshape(IT, 1, CH),
        "down_w": put(a["L0_ffn_down_w"].reshape(IT, P, DM)),
        "down_z": put(a["L0_ffn_down_z"].reshape(IT, 1, DM)),
        "down_s": put(a["L0_ffn_down_s"].reshape(IT, KT, P).transpose(2, 0, 1)),
    }
    nc = bacc.Bacc("TRN2", target_bir_lowering=False, num_devices=1, dynamic_dma_scratch_size=1024)
    d = {n: nc.dram_tensor(f"in_{n}", v.shape, mybir.dt.from_np(v.dtype), kind="ExternalInput").ap()
         for n, v in arrays.items()}
    outT = nc.dram_tensor("outT", (P, KT, TOK), F32, kind="ExternalOutput").ap()
    program(nc, d["x"], d["xT"], d["wq"], d["wkv"], d["wo"], d["slopes"], d["qkw"],
            (d["gate_w"], d["gate_z"], d["gate_s"]), (d["up_w"], d["up_z"], d["up_s"]),
            (d["down_w"], d["down_z"]), d["down_s"], outT)
    r = run_bass_kernel_spmd(nc, [{f"in_{n}": v for n, v in arrays.items()}], core_ids=[0])
    got = r.results[0]["outT"]
    return put(got.transpose(1, 0, 2).reshape(DM, TOK).T).reshape(1, TOK, DM)
```

```python
from contextlib import ExitStack

import numpy as np

import concourse.bass as bass
from concourse import mybir

F32 = mybir.dt.float32
F32R = mybir.dt.float32r
I32 = mybir.dt.int32
ALU = mybir.AluOpType
ACT = mybir.ActivationFunctionType

P = 128
TOK, DM = 1024, 512
HEADS, GROUPS, HD = 32, 8, 128
PER = HEADS // GROUPS
HID = 1792
QT = TOK // P
KT = DM // P
IT = HID // P
CH = 512
NC = TOK // CH
CT = CH // P
LN_EPS, RMS_EPS = 1e-5, 1e-6
MASKED = -1e30

TILES = list(range(QT - 1, -1, -1))
BASE = [P if t == 4 else 0 for t in range(QT)]
CUTS = [[(0, 256)], [(0, 256)], [(0, 384)], [(0, 512)], [(0, 384), (384, 256)], [(0, 512), (512, 256)],
        [(0, 512), (512, 384)], [(0, 512), (512, 512)]]
PBUF = [(0, 1024), (1024, 896), (1920, 768), (2688, 640)]
PBUF_COLS = 3328

STEP = 384
DIAG = [2048 + 1664, 2048]
PT_COLS = 2048 + 1664 + 4 * STEP + STEP


def pt_range(c, kt):
    r = kt - CT * c
    if r < 0:
        return kt * CH, CH, 0
    q0 = min(r, 2) * P
    return DIAG[c] + r * STEP + q0, CH - q0, q0


def parts(t):
    return [(0, 4), (4, t - 3)] if t >= CT else [(0, t + 1)]


LOTS = [(t, n) for t in TILES for n in range(len(parts(t)))]
PARTS = ["ss0"] + LOTS[:LOTS.index((3, 0))] + ["ss1"] + LOTS[LOTS.index((3, 0)):]
LN_PARTS = QT + 1
assert len(PARTS) % 2 == 0


def place_in_head(h, key):
    i = PARTS.index(key)
    return i - 1 if isinstance(h, int) and h == HEADS - 1 and i > PARTS.index("ss1") else i


def part_no(h, key):
    return LN_PARTS + len(PARTS) * h + place_in_head(h, key)


def hi_no(h, key):
    return QT + len(LOTS) * h + LOTS.index(key)


def last_lot(t):
    return t, len(parts(t)) - 1


PRO = ["kv0", "kv1", "kv2", "kv3", "qc1_0"]


def group_order(first, last):
    out = []
    for j in range(PER):
        nx = (j + 1) % PER
        more = not (last and j == PER - 1)
        prev, w = not (first and j == 0), not (first and j < 2)
        out += [f"qc0_{j}"] + [f"v0_{j}"] * prev + [f"w0_{j}", f"w1_{j}"] * w
        out += [f"qc1_{nx}"] * more + [f"w2_{j}"] * w + [f"kv{j}"] * (not last)
        out += [f"v1_{j}"] + [f"w3_{j}"] * w
    return out


FIRST, STEADY, LAST = group_order(True, False), group_order(False, False), group_order(False, True)
EPI = ["w1", "w3", "v0_0", "w5", "w7", "w0", "w2", "w4", "w6"]


def split_by_act(name):
    return name[0] in "vq"


class Places:

    def __init__(self, kind, g=None):
        self.order = {"pro": PRO, "first": FIRST, "steady": STEADY, "last": LAST, "epi": EPI}[kind]
        hi = lambda names: sum(map(split_by_act, names))
        a, b = len(PRO), hi(PRO)
        if kind == "pro":
            self.a, self.b, self.parity = 0, 0, 0
            return
        if kind == "first":
            self.a, self.b, self.parity = a, b, a % 2
            return
        a, b = a + len(FIRST), b + hi(FIRST)
        self.parity = a % 2
        if kind == "epi":
            self.a, self.b = a + len(STEADY) * (GROUPS - 2) + len(LAST), b + hi(STEADY) * (GROUPS - 2) + hi(LAST)
            self.parity = self.a % 2
            return
        n, m = len(STEADY), hi(STEADY)
        self.a, self.b = g * n + (a - n), g * m + (b - m)

    def n(self, name, more=1):
        return self.a + (self.order.index(name) + more)

    def hi(self, name):
        i = self.order.index(name)
        return self.b + sum(map(split_by_act, self.order[:i + 1]))

    def bank(self, name):
        return (self.parity + self.order.index(name)) % 2


assert len(STEADY) % 2 == 0


def f(ap):
    return ap.bitcast(F32)


def staging(stage):
    col = lambda n: stage[:, n * CH:(n + 1) * CH]
    loads = {k: (col(n).bitcast(I32), col(n + 1).bitcast(I32), col(n + 2)) for k, n in (("gate", 0), ("up", 3))}
    return loads, {"gate": col(0), "up": col(3)}


def attention(nc, stack, keep, x, wq, wkv, wo, slopes, qkw, mats, down_sc):
    sb = lambda n, shape, dt=F32: stack.enter_context(nc.sbuf_tensor(n, shape, dt))
    sem = lambda n: stack.enter_context(nc.semaphore(n))
    xh, xl, s_acc = keep["xh"], keep["xl"], keep["s"]
    xs = s_acc[:, :].rearrange("p (i n) -> p i n", i=QT)
    sT = s_acc[:, :].rearrange("p (m n) -> p m n", m=KT)

    pt_h, pt_l = sb("pt_h", [P, PT_COLS], F32R), sb("pt_l", [P, PT_COLS], F32R)
    oT_h, oT_l = sb("oT_h", [P, PER, TOK], F32R), sb("oT_l", [P, PER, TOK], F32R)
    kT_h, kT_l = sb("kT_h", [P, TOK], F32R), sb("kT_l", [P, TOK], F32R)
    v_h, v_l = sb("v_h", [P, QT, HD], F32R), sb("v_l", [P, QT, HD], F32R)
    q_h, q_l = sb("q_h", [P, TOK], F32R), sb("q_l", [P, TOK], F32R)
    wq_h, wq_l = sb("wq_h", [P, KT, HD], F32R), sb("wq_l", [P, KT, HD], F32R)
    wkv_h, wkv_l = (keep[n][:, :].rearrange("p (k w) -> p k w", w=2 * HD) for n in ("w0_h", "w0_l"))
    wo_h, wo_l = sb("wo_h", [P, PER, DM], F32R), sb("wo_l", [P, PER, DM], F32R)
    wq_in, wo_in = sb("wq_in", [P, KT, HD]), sb("wo_in", [P, DM])
    kv = keep["stage"][:, 0:QT * 2 * HD].rearrange("p (k w) -> p k w", w=2 * HD)
    wkv_in = keep["stage"][:, QT * 2 * HD:].rearrange("p (k w) -> p k w", w=2 * HD)
    sq = sb("sq", [P, TOK])
    pb = sb("pb", [P, PBUF_COLS])
    rel = sb("rel", [P, TOK])
    junk = sb("junk", [P, HD])
    ident = sb("ident", [P, P])
    sl = sb("sl", [P, HEADS])
    qk_w = sb("qk_w", [P, 2])
    qk = sb("qk", [P, 1])
    cst = sb("cst", [P, 3])
    stats = sb("stats", [P, QT, 6])
    mv = sb("mv", [P, QT, 2])
    var_e = sb("var_e", [P, QT])
    rstd = sb("rstd", [P, QT])
    kss, kms, kinv = sb("kss", [P, QT]), sb("kms", [P, QT]), sb("kinv", [P, QT])
    ssum = sb("ssum", [P, QT])
    ms, root, inv, ninv, coef = (sb(n, [P, QT]) for n in ("ms", "root", "inv", "ninv", "coef"))
    low, rsum, rinv = sb("low", [P, QT]), sb("rsum", [P, QT]), sb("rinv", [P, QT])

    S = [stack.enter_context(nc.psum_tensor(f"S{n}", [P, 2 * CH], F32)) for n in range(2)]
    T = [stack.enter_context(nc.psum_tensor(f"T{n}", [P, CH], F32)) for n in range(2)]
    O = [stack.enter_context(nc.psum_tensor(f"O{n}", [P, CH], F32)) for n in range(2)]

    LN_BANKS = [T[0][:, :], T[1][:, :]] + [S[n // 2][:, n % 2 * CH:(n % 2 + 1) * CH] for n in range(4)]

    x_in = [sem(f"x_in{i}") for i in range(QT)]
    tab_in = sem("tab_in")
    wq_ld, wkv_ld, wo_ld = sem("wq_ld"), sem("wkv_ld"), sem("wo_ld")
    wq_split, wkv_split, wo_split = sem("wq_split"), sem("wkv_split"), sem("wo_split")
    setup, ln_st, ln_mv, ln_var, ln_rstd, xn_ready = (
        sem("setup"), sem("ln_st"), sem("ln_mv"), sem("ln_var"), sem("ln_rstd"), sem("xn_ready"))
    sT_zero, qk_ready = sem("sT_zero"), sem("qk_ready")
    tr_ready, tr_hi, tr_lo = sem("tr_ready"), sem("tr_hi"), sem("tr_lo")
    out_ready, out_hi, out_free = sem("out_ready"), sem("out_hi"), sem("out_free")
    kss_ready, kms_ready, kinv_ready, kn_ready, v_ready = (
        sem("kss_ready"), sem("kms_ready"), sem("kinv_ready"), sem("kn_ready"), sem("v_ready"))
    kt_ready, kt_hi, kt_lo = sem("kt_ready"), sem("kt_hi"), sem("kt_lo")
    ms_ready = sem("ms_ready")
    root_ready, coef_ready = sem("root_ready"), sem("coef_ready")
    bias_ready, scores_ready, logits_ready = sem("bias_ready"), sem("scores_ready"), sem("logits_ready")
    exps_ready, rinv_ready, probs_ready = sem("exps_ready"), sem("rinv_ready"), sem("probs_ready")
    wq_hi, wkv_hi, wo_hi, v_hi_done = sem("wq_hi"), sem("wkv_hi"), sem("wo_hi"), sem("v_hi_done")
    SETUP = 6

    ffn_in, ffn_f = staging(keep["stage"])
    slot = {"gate": slice(0, CH), "up": slice(CH, 2 * CH)}
    ffn_ld, ffn_diff, ffn_scaled, ffn_hi, ffn_ready = (
        {k: keep[f"{k}_{n}"] for k in ffn_in} for n in ("ld", "diff", "scaled", "w_hi", "w_ready"))

    def pbuf(idx, t):
        a, w = PBUF[idx % 4]
        return pb[:, a:a + (t + 1) * P]

    def pt_lot(pt, t, n):
        k0, m = parts(t)[n]
        c, ql = t // CT, t % CT
        if k0 == 0 and c == 1:
            return pt[:, 0:4 * CH].rearrange("p (k w) -> p k w", w=CH)[:, :, ql * P:(ql + 1) * P]
        a = DIAG[c] + ql * P
        return pt[:, a:a + m * STEP].rearrange("p (k w) -> p k w", w=STEP)[:, :, 0:P]

    block = stack.enter_context(nc.Block())

    @block.sync
    def _(sp):
        for i in range(QT):
            sp.dma_start(xs[:, i, :], x[i]).then_inc(x_in[i], 16)
            if i == CT - 1:
                sp.dma_start(wkv_in[:, :, :], wkv[0]).then_inc(wkv_ld, 16)
        sp.dma_start(wq_in[:, :, :], wq[0]).then_inc(wq_ld, 16)
        sp.dma_start(sl[:, :], slopes).then_inc(tab_in, 16)
        sp.dma_start(qk_w[:, :], qkw).then_inc(tab_in, 16)
        sp.dma_start(wo_in[:, :], wo[0]).then_inc(wo_ld, 16)
        sp.dma_start(keep["dsc"][:, :, :], down_sc).then_inc(keep["dsc_in"], 16)


        def group(g, last=False):
            for j in range(PER):
                h = g * PER + j
                if last and j == 1:
                    sp.wait_ge(v_ready, GROUPS)
                    sp.wait_ge(wkv_split, GROUPS)
                    ffn_load(0)
                if j == 0 and not last:
                    sp.wait_ge(wkv_split, g + 1)
                    sp.dma_start(wkv_in[:, :, :], wkv[g + 1]).then_inc(wkv_ld, 16)
                if not (last and j == PER - 1):
                    sp.wait_ge(wq_split, h + 1)
                    sp.dma_start(wq_in[:, :, :], wq[h + 1]).then_inc(wq_ld, 16)
                    sp.wait_ge(wo_split, h + 1)
                    sp.dma_start(wo_in[:, :], wo[h + 1]).then_inc(wo_ld, 16)

        def ffn_load(i):
            for k, (w_i, z_i, s_i) in ffn_in.items():
                w, z, s = (m[i] for m in mats[k])
                sp.dma_start(w_i, w).then_inc(ffn_ld[k], 16)
                sp.dma_start(z_i, z.to_broadcast([P, CH])).then_inc(ffn_ld[k], 16)
                sp.dma_start(s_i, s.to_broadcast([P, CH])).then_inc(ffn_ld[k], 16)

        group(0)
        with sp.Fori(1, GROUPS - 1) as g:
            group(g)
        group(GROUPS - 1, last=True)
        for k in ffn_in:
            sp.wait_ge(ffn_ready[k], 1)
        ffn_load(1)

    @block.gpsimd
    def _(pool):
        g_ = nc.gpsimd
        g_.memset(cst[:, 0:1], -0.5).then_inc(setup, 1)
        g_.memset(cst[:, 1:2], 0.5).then_inc(setup, 1)
        g_.memset(cst[:, 2:3], -1.0).then_inc(setup, 1)
        g_.memset(ident[:, :], 0.0).then_inc(setup, 1)
        g_.iota(rel[:, :], pattern=[[1, TOK]], base=-(TOK - P), channel_multiplier=-1,
                allow_small_or_imprecise_dtypes=True).then_inc(setup, 1)
        pool.wait_ge(setup, 5)
        g_.affine_select(out=ident[:, :], in_=ident[:, :], compare_op=ALU.not_equal, fill=1.0, base=0,
                         pattern=[[-1, P]], channel_multiplier=1).then_inc(setup, 1)
        g_.affine_select(out=rel[:, :], in_=rel[:, :], compare_op=ALU.is_ge, fill=MASKED, base=TOK - P,
                         pattern=[[-1, TOK]], channel_multiplier=1).then_inc(setup, 1)
        for c in range(NC):
            a, _, _ = pt_range(c, CT * c + 3)
            for pt in (pt_h, pt_l):
                g_.memset(f(pt[:, a:a + P]), 0.0).then_inc(setup, 1)

        def lo_part(lo, src, hi, hi_done, done, n):
            pool.wait_ge(hi_done, n + 1)
            g_.tensor_tensor(lo, src, f(hi), ALU.subtract).then_inc(done, 1)

        def wq_lo(h):
            lo_part(wq_l[:, :, :], wq_in[:, :, :], wq_h[:, :, :], wq_hi, wq_split, h)

        def wkv_lo(g):
            lo_part(wkv_l[:, :, :], wkv_in[:, :, :], wkv_h[:, :, :], wkv_hi, wkv_split, g)

        def wo_lo(h, j):
            lo_part(wo_l[:, j, :], wo_in[:, :], wo_h[:, j, :], wo_hi, wo_split, h)

        def norms(h, c):
            cs = slice(c * CT, (c + 1) * CT)
            n = h * 2 + (1 - c)
            pool.wait_ge(ms_ready, n + 1)
            half = lambda k: cst[:, k:k + 1].to_broadcast([P, CT])
            g_.tensor_tensor(root[:, cs], ms[:, cs], half(1), ALU.pow).then_inc(root_ready, 1)
            g_.tensor_tensor(inv[:, cs], ms[:, cs], half(0), ALU.pow).then_inc(root_ready, 1)
            pool.wait_ge(root_ready, n * 2 + 2)
            g_.tensor_tensor(ninv[:, cs], inv[:, cs], half(2), ALU.mult).then_inc(coef_ready, 1)
            slope = sl[:, bass.ds(h, 1)] if not isinstance(h, int) else sl[:, h:h + 1]
            g_.tensor_tensor(coef[:, cs], root[:, cs], slope.to_broadcast([P, CT]),
                             ALU.mult).then_inc(coef_ready, 1)

        def bias(h, idx):
            t = TILES[idx]
            c = t // CT
            pool.wait_ge(coef_ready, h * 4 + (2 - c) * 2)
            if idx < 4:
                if not (isinstance(h, int) and h == 0):
                    prev = TILES[idx + 4]
                    pool.wait_ge(tr_ready, part_no(h - 1, last_lot(prev)) + 1)
            else:
                prev = TILES[idx - 4]
                pool.wait_ge(tr_ready, part_no(h, last_lot(prev)) + 1)
            w = (t + 1) * P
            g_.tensor_tensor(pbuf(idx, t), rel[:, TOK - w:TOK], coef[:, t:t + 1].to_broadcast([P, w]),
                             ALU.mult).then_inc(bias_ready, 1)

        def k_norm(g):
            pool.wait_ge(kms_ready, g + 1)
            g_.tensor_tensor(kinv[:, :], kms[:, :], cst[:, 0:1].to_broadcast([P, QT]),
                             ALU.pow).then_inc(kinv_ready, 1)
            pool.wait_ge(kinv_ready, g + 1)
            g_.tensor_tensor(kv[:, :, 0:HD], kv[:, :, 0:HD],
                             kinv[:, :].rearrange("p (k o) -> p k o", o=1).to_broadcast([P, QT, HD]),
                             ALU.mult).then_inc(kn_ready, 1)

        pool.wait_ge(setup, SETUP + 5)
        for c in range(NC):
            cs = slice(c * CT, (c + 1) * CT)
            pool.wait_ge(ln_var, c + 1)
            g_.tensor_tensor(rstd[:, cs], var_e[:, cs], cst[:, 0:1].to_broadcast([P, CT]), ALU.pow).then_inc(ln_rstd, 1)
            if c == 0:
                wkv_lo(0)
        wq_lo(0)
        pool.wait_ge(tr_ready, QT)
        g_.memset(s_acc[:, :], 0.0).then_inc(sT_zero, 1)
        pool.wait_ge(tab_in, 32)
        k_norm(0)
        norms(0, 1)
        bias(0, 0)
        bias(0, 1)

        def group(g, kind):
            at = Places(kind, g)
            last = kind == "last"
            for j in range(PER):
                h = g * PER + j
                more = not (last and j == PER - 1)
                bias(h, 2)
                bias(h, 3)
                if j == 0 and not last:
                    wkv_lo(g + 1)
                wo_lo(h, j)
                if more:
                    wq_lo(h + 1)
                norms(h, 0)
                if j == 0:
                    lo_part(v_l[:, :, :], kv[:, :, HD:2 * HD], v_h[:, :, :], v_hi_done, v_ready, g)
                bias(h, 4)
                bias(h, 5)
                bias(h, 6)
                if last and j == 2:
                    for k in ffn_in:
                        pool.wait_ge(ffn_diff[k], 1)
                        g_.tensor_tensor(ffn_f[k], ffn_f[k], ffn_in[k][2], ALU.mult).then_inc(ffn_scaled[k], 1)
                if last and j == 3:
                    for k in ffn_in:
                        pool.wait_ge(ffn_hi[k], 1)
                        g_.tensor_tensor(keep["w0_l"][:, slot[k]], ffn_f[k], f(keep["w0_h"][:, slot[k]]),
                                         ALU.subtract).then_inc(ffn_ready[k], 1)
                bias(h, 7)
                if j == PER - 1 and not last:
                    k_norm(g + 1)
                if more:
                    norms(h + 1, 1)
                    bias(h + 1, 0)
                    bias(h + 1, 1)

        group(0, "first")
        with pool.Fori(1, GROUPS - 1) as g:
            group(g, "steady")
        group(GROUPS - 1, "last")

    @block.scalar
    def _(act):
        a_ = nc.scalar

        def lot(h, t, n):
            m = parts(t)[n][1]
            act.wait_ge(tr_ready, part_no(h, (t, n)) + 1)
            bank = T[place_in_head(h, (t, n)) % 2]
            a_.activation(pt_lot(pt_h, t, n), bank[:, 0:m * P].rearrange("p (k w) -> p k w", w=P),
                          ACT.Copy).then_inc(tr_hi, 1)

        def lots(h, t):
            for n in range(len(parts(t))):
                lot(h, t, n)

        def exp(h, idx):
            t = TILES[idx]
            act.wait_ge(logits_ready, h * QT + (idx + 1))
            a_.activation(pbuf(idx, t), pbuf(idx, t), ACT.Exp, bias=low[:, idx:idx + 1], scale=-1.0,
                          accum_out=rsum[:, idx:idx + 1]).then_inc(exps_ready, 1)

        def q_hi(at, name):
            cs = slice(CH * (name[2] == "1"), CH * (name[2] == "1") + CH)
            act.wait_ge(out_ready, at.n(name))
            a_.activation(q_h[:, cs], O[at.bank(name)][:, :], ACT.Copy)
            a_.activation(sq[:, cs], O[at.bank(name)][:, :], ACT.Square).then_inc(out_hi, 1)

        def v_hi(at, name, j):
            cs = slice(CH * (name[1] == "1"), CH * (name[1] == "1") + CH)
            act.wait_ge(out_ready, at.n(name))
            a_.activation(oT_h[:, j, cs], O[at.bank(name)][:, :], ACT.Copy).then_inc(out_hi, 1)

        def k_squares(at, names, g):
            for name in names:
                act.wait_ge(out_free, at.n(name))
                for k in (2 * int(name[2]), 2 * int(name[2]) + 1):
                    if not (isinstance(g, int) and g * QT + k == 0):
                        act.wait_ge(kss_ready, g * QT + k)
                    a_.activation(junk[:, :], kv[:, k, 0:HD], ACT.Square,
                                  accum_out=kss[:, k:k + 1]).then_inc(kss_ready, 1)

        def wq_hi_part(h):
            act.wait_ge(wq_ld, h * 16 + 16)
            a_.activation(wq_h[:, :, :], wq_in[:, :, :], ACT.Copy).then_inc(wq_hi, 1)

        def wkv_hi_part(g):
            act.wait_ge(wkv_ld, g * 16 + 16)
            a_.activation(wkv_h[:, :, :], wkv_in[:, :, :], ACT.Copy).then_inc(wkv_hi, 1)

        def wo_hi_part(h, j):
            act.wait_ge(wo_ld, h * 16 + 16)
            a_.activation(wo_h[:, j, :], wo_in[:, :], ACT.Copy).then_inc(wo_hi, 1)

        wkv_hi_part(0)
        wq_hi_part(0)
        for i in range(QT):
            act.wait_ge(tr_ready, i + 1)
            a_.activation(xh[:, :, i * P:(i + 1) * P], LN_BANKS[i % 6].rearrange("p (k w) -> p k w", w=P),
                          ACT.Copy).then_inc(tr_hi, 1)
        pro = Places("pro")
        k_squares(pro, ["kv0", "kv1", "kv2", "kv3"], 0)
        q_hi(pro, "qc1_0")

        def group(g, kind):
            at = Places(kind, g)
            act.wait_ge(qk_ready, 1)
            act.wait_ge(kt_ready, g + 1)
            a_.activation(kT_h[:, :], S[0][:, :], ACT.Copy, scale=qk[:, 0:1]).then_inc(kt_hi, 1)
            for j in range(PER):
                h = g * PER + j
                more = not (kind == "last" and j == PER - 1)
                prev = not (kind == "first" and j == 0)
                if prev:
                    lots(h - 1, 1)
                    lots(h - 1, 0)
                if j > 0:
                    exp(h, 0)
                elif kind != "last":
                    wkv_hi_part(g + 1)
                q_hi(at, f"qc0_{j}")
                if j == 0:
                    exp(h, 0)
                exp(h, 1)
                if prev:
                    v_hi(at, f"v0_{j}", (j - 1) % PER)
                lots(h, 7)
                wo_hi_part(h, j)
                if more:
                    wq_hi_part(h + 1)
                exp(h, 2)
                lots(h, 6)
                if j == 0:
                    a_.activation(v_h[:, :, :], kv[:, :, HD:2 * HD], ACT.Copy).then_inc(v_hi_done, 1)
                lot(h, 5, 0)
                exp(h, 3)
                lot(h, 5, 1)
                if more:
                    q_hi(at, f"qc1_{(j + 1) % PER}")
                lot(h, 4, 0)
                exp(h, 4)
                lot(h, 4, 1)
                exp(h, 5)
                if kind != "last":
                    k_squares(at, [f"kv{j}"], g + 1)
                exp(h, 6)
                lots(h, 3)
                lots(h, 2)
                v_hi(at, f"v1_{j}", j)
                exp(h, 7)
                if kind == "last" and j == 2:
                    for k in ffn_in:
                        act.wait_ge(ffn_scaled[k], 1)
                        a_.activation(keep["w0_h"][:, slot[k]], ffn_f[k], ACT.Copy).then_inc(ffn_hi[k], 1)

        group(0, "first")
        with act.Fori(1, GROUPS - 1) as g:
            group(g, "steady")
        group(GROUPS - 1, "last")
        lots(HEADS - 1, 1)
        lots(HEADS - 1, 0)
        v_hi(Places("epi"), "v0_0", PER - 1)

    @block.vector
    def _(dve):
        v_ = nc.vector
        def ln_stats(tiles):
            for i in tiles:
                dve.wait_ge(x_in[i], 16)
                v_.bn_stats(stats[:, i, :], xs[:, i, :]).then_inc(ln_st, 1)

        def ln_variance(c):
            tiles = range(c * CT, (c + 1) * CT)
            for i in tiles:
                dve.wait_ge(ln_st, i + 1)
                v_.bn_aggr(mv[:, i, :], stats[:, i, :]).then_inc(ln_mv, 1)
            dve.wait_ge(ln_mv, (c + 1) * CT)
            cs = slice(c * CT, (c + 1) * CT)
            v_.tensor_scalar(var_e[:, cs], mv[:, cs, 1], LN_EPS, None, ALU.add).then_inc(ln_var, 1)

        def ln_normalise(tiles):
            for i in tiles:
                dve.wait_ge(ln_rstd, i // CT + 1)
                v_.tensor_scalar(xs[:, i, :], xs[:, i, :], mv[:, i, 0:1], rstd[:, i:i + 1], ALU.subtract,
                                 ALU.mult).then_inc(xn_ready, 1)

        def ln_lo(tiles):
            for i in tiles:
                dve.wait_ge(tr_hi, i + 1)
                cs = slice(i * P, (i + 1) * P)
                v_.tensor_tensor(xl[:, :, cs], LN_BANKS[i % 6].rearrange("p (k w) -> p k w", w=P),
                                 f(xh[:, :, cs]), ALU.subtract).then_inc(tr_lo, 1)

        ln_stats(range(0, 4))
        ln_variance(0)
        ln_stats(range(4, 6))
        ln_normalise(range(0, 4))
        ln_stats(range(6, 8))
        ln_variance(1)
        ln_lo(range(0, 2))
        ln_normalise(range(4, 6))
        ln_lo(range(2, 4))
        ln_normalise(range(6, 8))
        ln_lo(range(4, 6))

        def lot(h, t, n):
            m = parts(t)[n][1]
            dve.wait_ge(tr_hi, hi_no(h, (t, n)) + 1)
            bank = T[place_in_head(h, (t, n)) % 2]
            v_.tensor_tensor(pt_lot(pt_l, t, n), bank[:, 0:m * P].rearrange("p (k w) -> p k w", w=P),
                             f(pt_lot(pt_h, t, n)), ALU.subtract).then_inc(tr_lo, 1)

        def lots(h, t):
            for n in range(len(parts(t))):
                lot(h, t, n)

        def logits(h, idx):
            t = TILES[idx]
            n = h * QT + (idx + 1)
            dve.compute_val(n)
            dve.wait_ge(setup, SETUP + 5)
            dve.wait_ge(bias_ready, n)
            dve.wait_ge(scores_ready, n)
            v_.tensor_tensor_reduce(out=pbuf(idx, t), in0=S[idx % 2][:, BASE[t]:BASE[t] + (t + 1) * P],
                                    in1=pbuf(idx, t), scale=ninv[:, t:t + 1], scalar=3e38, op0=ALU.add,
                                    op1=ALU.min, accum_out=low[:, idx:idx + 1]).then_inc(logits_ready, 1)

        def normalise(h, idx):
            dve.wait_ge(exps_ready, h * QT + (idx + 1))
            v_.reciprocal(rinv[:, idx:idx + 1], rsum[:, idx:idx + 1]).then_inc(rinv_ready, 1)
            t = TILES[idx]
            dve.wait_ge(rinv_ready, h * QT + (idx + 1))
            v_.tensor_scalar(pbuf(idx, t), pbuf(idx, t), rinv[:, idx:idx + 1], None, ALU.mult
                             ).then_inc(probs_ready, 1)

        def q_lo(at, name):
            cs = slice(CH * (name[2] == "1"), CH * (name[2] == "1") + CH)
            dve.wait_ge(out_hi, at.hi(name))
            v_.tensor_tensor(q_l[:, cs], O[at.bank(name)][:, :], f(q_h[:, cs]), ALU.subtract).then_inc(out_free, 1)

        def v_lo(at, name, j):
            cs = slice(CH * (name[1] == "1"), CH * (name[1] == "1") + CH)
            dve.wait_ge(out_hi, at.hi(name))
            v_.tensor_tensor(oT_l[:, j, cs], O[at.bank(name)][:, :], f(oT_h[:, j, cs]),
                             ALU.subtract).then_inc(out_free, 1)

        def mean_sq(h, c, part, bank):
            cs = slice(c * CT, (c + 1) * CT)
            n = h * 2 + (2 - c)
            dve.wait_ge(tr_ready, part + 1)
            v_.tensor_reduce(out=ssum[:, cs], in_=bank[:, :].rearrange("p (k w) -> p k w", w=P),
                             axis=mybir.AxisListType.X, op=ALU.add).then_inc(tr_lo, 1)
            dve.wait_ge(tr_lo, part + 1)
            v_.tensor_scalar(ms[:, cs], ssum[:, cs], HD * RMS_EPS, None, ALU.add).then_inc(ms_ready, 1)

        def kv_copy(at, names, g):
            for name in names:
                k = 2 * int(name[2])
                dve.wait_ge(v_ready, g)
                dve.wait_ge(out_ready, at.n(name))
                v_.tensor_copy(kv[:, k:k + 2, :], O[at.bank(name)][:, :].rearrange("p (k w) -> p k w", w=2 * HD)
                               ).then_inc(out_free, 1)

        def k_mean_sq(g):
            dve.wait_ge(kss_ready, g * QT + QT)
            v_.tensor_scalar(kms[:, :], kss[:, :], 1.0 / HD, RMS_EPS, ALU.mult, ALU.add).then_inc(kms_ready, 1)

        def project(at, name, unit):
            m, c = divmod(unit, NC)
            dst = sT[:, m, c * CH:(c + 1) * CH]
            dve.wait_ge(out_ready, at.n(name))
            v_.tensor_tensor(dst, O[at.bank(name)][:, :], dst, ALU.add).then_inc(out_free, 1)

        pro = Places("pro")
        for n in range(4):
            if n == 1:
                ln_lo(range(6, 8))
                dve.wait_ge(tab_in, 32)
                v_.tensor_tensor(qk[:, :], qk_w[:, 0:1], qk_w[:, 1:2], ALU.mult).then_inc(qk_ready, 1)
            dve.wait_ge(out_ready, pro.n(f"kv{n}"))
            v_.tensor_copy(kv[:, 2 * n:2 * n + 2, :], O[pro.bank(f"kv{n}")][:, :].rearrange("p (k w) -> p k w", w=2 * HD)
                           ).then_inc(out_free, 1)
        k_mean_sq(0)
        q_lo(pro, "qc1_0")
        mean_sq(0, 1, QT, T[1])
        dve.wait_ge(sT_zero, 1)

        def group(g, kind):
            at = Places(kind, g)
            last = kind == "last"
            if kind != "first":
                normalise(g * PER - 1, 7)
            dve.wait_ge(kt_hi, g + 1)
            v_.scalar_tensor_tensor(out=kT_l[:, :], in0=S[0][:, :], scalar=qk[:, 0:1], in1=f(kT_h[:, :]),
                                    op0=ALU.mult, op1=ALU.subtract).then_inc(kt_lo, 1)
            for j in range(PER):
                h = g * PER + j
                nx = (j + 1) % PER
                more = not (last and j == PER - 1)
                prev = not (kind == "first" and j == 0)
                w = not (kind == "first" and j < 2)
                unit = 4 * (j % 2)
                if prev and j > 0:
                    normalise(h - 1, 7)
                if j > 0:
                    logits(h, 0)
                if prev:
                    lots(h - 1, 1)
                    lots(h - 1, 0)
                if j > 0:
                    normalise(h, 0)
                    logits(h, 1)
                    q_lo(at, f"qc0_{j}")
                else:
                    logits(h, 0)
                    q_lo(at, f"qc0_{j}")
                    logits(h, 1)
                if j == 0:
                    normalise(h, 0)
                mean_sq(h, 0, part_no(h, "ss0"), T[0])
                normalise(h, 1)
                if prev:
                    v_lo(at, f"v0_{j}", (j - 1) % PER)
                lot(h, 7, 0)
                logits(h, 2)
                lot(h, 7, 1)
                if w:
                    project(at, f"w0_{j}", unit)
                normalise(h, 2)
                lot(h, 6, 0)
                if w:
                    project(at, f"w1_{j}", unit + 1)
                lot(h, 6, 1)
                logits(h, 3)
                lot(h, 5, 0)
                normalise(h, 3)
                lot(h, 5, 1)
                logits(h, 4)
                if more:
                    q_lo(at, f"qc1_{nx}")
                else:
                    project(at, f"w2_{j}", unit + 2)
                lot(h, 4, 0)
                normalise(h, 4)
                if w and more:
                    project(at, f"w2_{j}", unit + 2)
                lot(h, 4, 1)
                logits(h, 5)
                normalise(h, 5)
                if not last:
                    kv_copy(at, [f"kv{j}"], g + 1)
                if more:
                    mean_sq(h + 1, 1, part_no(h, "ss1"), T[place_in_head(h, "ss1") % 2])
                logits(h, 6)
                if j == PER - 1 and not last:
                    k_mean_sq(g + 1)
                lots(h, 3)
                normalise(h, 6)
                lots(h, 2)
                v_lo(at, f"v1_{j}", j)
                if w:
                    project(at, f"w3_{j}", unit + 3)
                logits(h, 7)
                if last and j == 1:
                    for k, (w_i, z_i, _) in ffn_in.items():
                        dve.wait_ge(ffn_ld[k], 48)
                        v_.tensor_tensor(ffn_f[k], w_i, z_i, ALU.subtract).then_inc(ffn_diff[k], 1)

        group(0, "first")
        with dve.Fori(1, GROUPS - 1) as g:
            group(g, "steady")
        group(GROUPS - 1, "last")
        epi = Places("epi")
        normalise(HEADS - 1, 7)
        project(epi, "w1", 1)
        lots(HEADS - 1, 1)
        project(epi, "w3", 3)
        lots(HEADS - 1, 0)
        v_lo(epi, "v0_0", PER - 1)
        for name in EPI[3:]:
            project(epi, name, int(name[1]))

    @block.tensor
    def _(pe):
        mm = nc.tensor.matmul

        def products(out, terms, between=None, done=0):
            n = 0
            for ah, al, bh, bl in terms:
                for a, b in ((ah, bh), (ah, bl), (al, bh)):
                    ins = mm(out, a, b, start=(n == 0), stop=(n == 3 * len(terms) - 1))
                    n += 1
                    for work in (between or {}).get(done + n, ()):
                        work()
            return ins

        def take(at, name):
            first2 = at.order is PRO and at.order.index(name) < 2
            if not first2:
                pe.wait_ge(out_free, at.n(name, more=-1))
            return O[at.bank(name)]

        def lot(h, t, n):
            idx = TILES.index(t)
            k0, m = parts(t)[n]
            no = part_no(h, (t, n))
            pe.wait_ge(probs_ready, h * QT + (idx + 1))
            pe.wait_ge(tr_lo, no - 1)
            bank = T[place_in_head(h, (t, n)) % 2]
            for k in range(m):
                ins = nc.tensor.transpose(bank[:, k * P:(k + 1) * P],
                                          pbuf(idx, t)[:, (k0 + k) * P:(k0 + k + 1) * P], ident[:, :])
            ins.then_inc(tr_ready, 1)

        def lots(h, t):
            for n in range(len(parts(t))):
                lot(h, t, n)

        def scores(h, idx):
            t = TILES[idx]
            if not (isinstance(h, int) and h == 0 and idx < 2):
                pe.wait_ge(logits_ready, h * QT + (idx - 1))
            bank = S[idx % 2]
            qs = slice(t * P, (t + 1) * P)
            cuts = CUTS[t]
            for q, last in ((q_h, False), (q_l, True)):
                for k0, w in cuts:
                    out = bank[:, BASE[t] + k0:BASE[t] + k0 + w]
                    if not last:
                        mm(out, q[:, qs], kT_h[:, k0:k0 + w], start=True, stop=False)
                        mm(out, q[:, qs], kT_l[:, k0:k0 + w], start=False, stop=False)
                    else:
                        ins = mm(out, q[:, qs], kT_h[:, k0:k0 + w], start=False, stop=True)
            ins.then_inc(scores_ready, 1)

        def values(at, name, h, wait, between=None):
            c = int(name[1])
            out = take(at, name)
            last_t = c * CT
            pe.wait_ge(tr_lo, part_no(h, last_lot(last_t)) + 1)
            if wait is not None:
                pe.wait_ge(v_ready, wait)
            n = CT * (c + 1)
            for kt in range(n):
                a, w, q0 = pt_range(c, kt)
                o = out[:, q0:q0 + w]
                for i, (v, pt) in enumerate(((v_h, pt_h), (v_h, pt_l), (v_l, pt_h))):
                    ins = mm(o, v[:, kt, :], pt[:, a:a + w], start=(kt + i == 0), stop=(kt == n - 1 and i == 2))
                    for work in (between or {}).get(3 * kt + i + 1, ()):
                        work()
            ins.then_inc(out_ready, 1)

        def q_proj(at, name, h, between=None):
            c = int(name[2])
            out = take(at, name)
            pe.wait_ge(wq_split, h + 1)
            cs = slice(c * CH, (c + 1) * CH)
            products(out[:, :], [(wq_h[:, k, :], wq_l[:, k, :], xh[:, k, cs], xl[:, k, cs]) for k in range(KT)],
                     between).then_inc(out_ready, 1)

        def squares(hi, c, part, bank):
            pe.wait_ge(out_hi, hi)
            pe.wait_ge(tr_lo, part - 1)
            for k in range(CT):
                a = (c * CT + k) * P
                ins = nc.tensor.transpose(bank[:, k * P:(k + 1) * P], sq[:, a:a + P], ident[:, :])
            ins.then_inc(tr_ready, 1)

        def kv_proj(at, name, g, between=None):
            out = take(at, name)
            pe.wait_ge(wkv_split, g + 1)
            for i in range(2):
                a = (2 * int(name[2]) + i) * P
                ins = products(out[:, i * 2 * HD:(i + 1) * 2 * HD],
                               [(xh[:, k, a:a + P], xl[:, k, a:a + P], wkv_h[:, k, :], wkv_l[:, k, :])
                                for k in range(KT)], between, i * 3 * KT)
            ins.then_inc(out_ready, 1)

        def k_transposes(g):
            pe.wait_ge(kn_ready, g + 1)
            if not (isinstance(g, int) and g == 0):
                pe.wait_ge(logits_ready, g * (PER * QT) - 1)
            for k in range(QT):
                ins = nc.tensor.transpose(S[0][:, k * P:(k + 1) * P], kv[:, k, 0:HD], ident[:, :])
            ins.then_inc(kt_ready, 1)

        def project(at, name, unit, h0, j0, outputs):
            m, c = divmod(unit, NC)
            out = take(at, name)
            pe.wait_ge(wo_split, h0 + 2)
            pe.wait_ge(out_free, outputs)
            ms_, cs = slice(m * P, (m + 1) * P), slice(c * CH, (c + 1) * CH)
            products(out[:, :], [(wo_h[:, j, ms_], wo_l[:, j, ms_], oT_h[:, j, cs], oT_l[:, j, cs])
                                 for j in (j0, j0 + 1)]).then_inc(out_ready, 1)

        pe.wait_ge(setup, SETUP + 5)
        pro = Places("pro")

        def ln_transposes(tiles):
            for i in tiles:
                pe.wait_ge(xn_ready, i + 1)
                if i >= 6:
                    pe.wait_ge(tr_lo, i - 5)
                for k in range(KT):
                    ins = nc.tensor.transpose(LN_BANKS[i % 6][:, k * P:(k + 1) * P],
                                              xs[:, i, k * P:(k + 1) * P], ident[:, :])
                ins.then_inc(tr_ready, 1)

        ln_transposes(range(0, 6))
        for n in range(4):
            pe.wait_ge(tr_lo, 2 * n + 2)
            kv_proj(pro, f"kv{n}", 0)
            if n == 0:
                ln_transposes(range(6, 8))
        q_proj(pro, "qc1_0", 0)

        def group(g, kind):
            at = Places(kind, g)
            last = kind == "last"
            if kind == "first":
                q_proj(at, "qc0_0", 0, {9: [lambda: squares(pro.hi("qc1_0"), 1, QT, T[1])]})
            k_transposes(g)
            for j in range(PER):
                h = g * PER + j
                nx = (j + 1) % PER
                more = not (last and j == PER - 1)
                prev = not (kind == "first" and j == 0)

                def w_unit(n, h=h, j=j):
                    if kind == "first" and j < 2:
                        return
                    project(at, f"w{n}_{j}", 4 * (j % 2) + n, h - 2 - j % 2, 0 if j >= 2 else 2,
                            at.n(f"v0_{j - j % 2}"))

                if j > 0:
                    scores(h, 0)
                if prev:
                    lots(h - 1, 1)
                if j > 0:
                    q_proj(at, f"qc0_{j}", h, {6: [lambda h=h: lots(h - 1, 0), lambda h=h: scores(h, 1)]})
                elif prev:
                    q_proj(at, f"qc0_{j}", h, {6: [lambda h=h: lots(h - 1, 0)]})
                if j == 0:
                    pe.wait_ge(kt_lo, g + 1)
                    scores(h, 0)
                    scores(h, 1)

                def squares0(h=h, j=j):
                    squares(at.hi(f"qc0_{j}"), 0, part_no(h, "ss0"), T[0])

                if prev:
                    values(at, f"v0_{j}", h - 1, None, {9: [squares0]})
                else:
                    squares0()
                lots(h, 7)
                scores(h, 2)
                w_unit(0)
                lot(h, 6, 0)
                w_unit(1)
                lot(h, 6, 1)
                scores(h, 3)
                lot(h, 5, 0)
                if more:
                    q_proj(at, f"qc1_{nx}", h + 1, {6: [lambda h=h: lot(h, 5, 1)]})
                else:
                    w_unit(2)
                    lot(h, 5, 1)
                scores(h, 4)
                lot(h, 4, 0)
                if more:
                    w_unit(2)
                lot(h, 4, 1)
                scores(h, 5)

                def squares1(h=h, nx=nx):
                    squares(at.hi(f"qc1_{nx}"), 1, part_no(h, "ss1"), T[place_in_head(h, "ss1") % 2])

                if not last:
                    kv_proj(at, f"kv{j}", g + 1, {3 * KT: [squares1]})
                elif more:
                    squares1()
                scores(h, 6)
                lots(h, 3)
                values(at, f"v1_{j}", h, g + 1 if j == 0 else None, {12: [lambda h=h: lots(h, 2)]})
                w_unit(3)
                scores(h, 7)

        group(0, "first")
        with pe.Fori(1, GROUPS - 1) as g:
            group(g, "steady")
        group(GROUPS - 1, "last")
        epi = Places("epi")
        v1_split = Places("last", GROUPS - 1).n(f"v1_{PER - 1}")

        def last_unit(name):
            unit = int(name[1])
            project(epi, name, unit, HEADS - 2, 2, v1_split if unit % NC else epi.n("v0_0"))

        last_unit("w1")
        lots(HEADS - 1, 1)
        last_unit("w3")
        lots(HEADS - 1, 0)
        values(epi, "v0_0", HEADS - 1, None)
        for name in EPI[3:]:
            last_unit(name)


def ffn(nc, stack, keep, xT, mats, outT):
    sb = lambda n, shape, dt=F32: stack.enter_context(nc.sbuf_tensor(n, shape, dt))
    sem = lambda n: stack.enter_context(nc.semaphore(n))
    xh, xl = keep["xh"], keep["xl"]
    sT = keep["s"][:, :].rearrange("p (m n) -> p m n", m=KT)
    yT = sb("yT", [P, KT, TOK])
    xt = sb("xt", [P, KT, TOK])
    KIND = ("gate", "up", "down")
    staged, w_f = staging(keep["stage"])
    staged["down"] = sb("down_in", [P, CH], I32)[:, :], sb("down_z", [P, CH], I32)[:, :]
    w_f["down"] = sb("down_f", [P, CH])[:, :]
    w_h = {k: [sb(f"{k}_h{n}", [P, CH], F32R)[:, :] for n in range(k != "down", 2)] for k in KIND}
    w_l = {k: [sb(f"{k}_l{n}", [P, CH], F32R)[:, :] for n in range(k != "down", 2)] for k in KIND}
    for n, k in enumerate(KIND[:2]):
        w_h[k].insert(0, keep["w0_h"][:, n * CH:(n + 1) * CH])
        w_l[k].insert(0, keep["w0_l"][:, n * CH:(n + 1) * CH])
    dsc = keep["dsc"]
    sg = [sb(f"sg{c}", [P, CH]) for c in range(NC)]
    hid = [sb(f"hid{c}", [P, CH]) for c in range(NC)]
    h_h = [sb(f"h_h{n}", [P, TOK], F32R) for n in range(2)]
    h_l = [sb(f"h_l{n}", [P, TOK], F32R) for n in range(2)]
    gate_ps = [stack.enter_context(nc.psum_tensor(f"gate_ps{c}", [P, CH], F32)) for c in range(NC)]
    up_ps = [stack.enter_context(nc.psum_tensor(f"up_ps{c}", [P, CH], F32)) for c in range(NC)]
    y_ps = [stack.enter_context(nc.psum_tensor(f"y_ps{n}", [P, CH], F32)) for n in range(4)]
    UNITS = KT * NC
    UNIT = [(m, c) for c in range(NC) for m in range(KT)]
    LAST = [(i, u) for half in (range(0, 4), range(4, 8)) for i in (IT - 2, IT - 1) for u in half]
    POOL_UNITS = 6

    ld, w_diff, w_hi, w_ready = ({k: keep[f"{k}_{n}"] for k in KIND} for n in ("ld", "diff", "w_hi", "w_ready"))
    w_scaled = {k: keep[f"{k}_scaled"] for k in KIND[:2]}
    dsc_in, xt_in = keep["dsc_in"], sem("xt_in")
    gate_ready, up_ready, sg_ready, hid_ready = sem("gate_ready"), sem("up_ready"), sem("sg_ready"), sem("hid_ready")
    h_hi, h_lo, y_ready, y_added = sem("h_hi"), sem("h_lo"), sem("y_ready"), sem("y_added")
    silu_ready, prod_ready, fin_by_pool, stored = sem("silu_ready"), sem("prod_ready"), sem("fin_by_pool"), sem("stored")
    fin_by_dve = sem("fin_by_dve")

    block = stack.enter_context(nc.Block())
    LOADS = {"gate": 3, "up": 3, "down": 2}

    @block.sync
    def _(sp):
        def load(k, i, first=False):
            if not first:
                sp.wait_ge(w_ready[k], i)
            sp.dma_start(staged[k][0], mats[k][0][i]).then_inc(ld[k], 16)
            sp.dma_start(staged[k][1], mats[k][1][i].to_broadcast([P, CH])).then_inc(ld[k], 16)
            if k != "down":
                sp.dma_start(staged[k][2], mats[k][2][i].to_broadcast([P, CH])).then_inc(ld[k], 16)

        load("down", 0, first=True)
        sp.dma_start(xt[:, :, :], xT).then_inc(xt_in, 16)
        load("down", 1)
        with sp.Fori(2, IT) as i:
            for k in KIND:
                load(k, i)
        for n, (m, c) in enumerate(UNIT):
            if n < POOL_UNITS:
                sp.wait_ge(fin_by_pool, n + 1)
            else:
                sp.wait_ge(fin_by_dve, n - POOL_UNITS + 1)
            sp.dma_start(outT[:, m, c * CH:(c + 1) * CH], xt[:, m, c * CH:(c + 1) * CH]).then_inc(stored, 16)
        sp.wait_ge(stored, 16 * UNITS)

    @block.gpsimd
    def _(pool):
        g_ = nc.gpsimd
        def scale(k, i):
            pool.wait_ge(w_diff[k], i + 1)
            g_.tensor_tensor(w_f[k], w_f[k], staged[k][2], ALU.mult).then_inc(w_scaled[k], 1)

        def weights(k, i, b):
            pool.wait_ge(w_hi[k], i + 1)
            g_.tensor_tensor(w_l[k][b][:, :], w_f[k], f(w_h[k][b][:, :]), ALU.subtract
                             ).then_inc(w_ready[k], 1)

        def hidden_lo(i, c, b):
            cs = slice(c * CH, (c + 1) * CH)
            pool.wait_ge(h_hi, i * NC + (c + 1))
            g_.tensor_tensor(h_l[b][:, cs], hid[c][:, :], f(h_h[b][:, cs]), ALU.subtract).then_inc(h_lo, 1)

        def step(i, b, first=False, last=False):
            if not last:
                scale("gate", i + 1)
                scale("up", i + 1)
            if not first:
                hidden_lo(i, 0, b)
            if not last:
                weights("gate", i + 1, 1 - b)
                weights("up", i + 1, 1 - b)
            if first:
                weights("down", i, b)
                hidden_lo(i, 0, b)
            hidden_lo(i, 1, b)
            if not last:
                weights("down", i + 1, 1 - b)

        step(0, 0, first=True)
        step(1, 1)
        with pool.Fori(1, IT // 2 - 1) as p:
            step(p * 2, 0)
            step(p * 2 + 1, 1)
        step(IT - 2, 0)
        step(IT - 1, 1, last=True)
        pool.wait_ge(xt_in, 16)
        for n, (m, c) in enumerate(UNIT[:POOL_UNITS]):
            cs = slice(c * CH, (c + 1) * CH)
            pool.wait_ge(prod_ready, n + 1)
            g_.tensor_tensor(xt[:, m, cs], xt[:, m, cs], yT[:, m, cs], ALU.add).then_inc(fin_by_pool, 1)

    @block.scalar
    def _(act):
        a_ = nc.scalar

        def weights(k, i, b, wait=None):
            act.wait_ge(w_diff[k] if k == "down" else w_scaled[k], i + 1)
            if wait is not None:
                act.wait_ge(*wait)
            a_.activation(w_h[k][b][:, :], w_f[k], ACT.Copy).then_inc(w_hi[k], 1)

        def step(i, b, first=False, last=False):
            if first:
                weights("gate", i + 1, 1 - b)
                weights("up", i + 1, 1 - b)
                weights("down", i, b)
            for c in range(NC):
                cs = slice(c * CH, (c + 1) * CH)
                act.wait_ge(gate_ready, i * NC + (c + 1))
                if not first:
                    act.wait_ge(hid_ready, i * NC + (c - 1))
                a_.activation(sg[c][:, :], gate_ps[c][:, :], ACT.Silu).then_inc(sg_ready, 1)
                act.wait_ge(hid_ready, i * NC + (c + 1))
                if not (first):
                    act.wait_ge(y_ready, (i - 1) * UNITS)
                a_.activation(h_h[b][:, cs], hid[c][:, :], ACT.Copy).then_inc(h_hi, 1)
                if last:
                    continue
                if c == 0 and not first:
                    weights("gate", i + 1, 1 - b, (gate_ready, i * NC))
                    weights("up", i + 1, 1 - b, (up_ready, i * NC))
                elif c == 1:
                    weights("down", i + 1, 1 - b, None if first else (y_ready, i * UNITS))

        step(0, 0, first=True)
        step(1, 1)
        with act.Fori(1, IT // 2 - 1) as p:
            step(p * 2, 0)
            step(p * 2 + 1, 1)
        step(IT - 2, 0)
        step(IT - 1, 1, last=True)
        for n, (m, c) in enumerate(UNIT):
            cs = slice(c * CH, (c + 1) * CH)
            act.wait_ge(y_added, UNITS * (IT - 2) + LAST.index((IT - 1, n)) + 1)
            a_.activation(yT[:, m, cs], yT[:, m, cs], ACT.Silu).then_inc(silu_ready, 1)

    @block.vector
    def _(dve):
        v_ = nc.vector
        def hidden(i, c, first=False):
            dve.wait_ge(sg_ready, i * NC + (c + 1))
            dve.wait_ge(up_ready, i * NC + (c + 1))
            if not first:
                dve.wait_ge(h_lo, i * NC + (c - 1))
            v_.tensor_tensor(hid[c][:, :], sg[c][:, :], up_ps[c][:, :], ALU.mult).then_inc(hid_ready, 1)

        def add(i, units):
            for u in units:
                m, c = UNIT[u]
                dst = yT[:, m, c * CH:(c + 1) * CH]
                sc = dsc[:, i, m:m + 1] if isinstance(i, int) else dsc[:, bass.ds(i, 1), m]
                dve.wait_ge(y_ready, i * UNITS + (u + 1))
                if isinstance(i, int) and i == 0:
                    v_.tensor_scalar(dst, y_ps[u % 4][:, :], sc, None, ALU.mult).then_inc(y_added, 1)
                    continue
                dve.wait_ge(y_added, (i - 1) * UNITS + (u + 1))
                v_.scalar_tensor_tensor(out=dst, in0=y_ps[u % 4][:, :], scalar=sc, in1=dst, op0=ALU.mult,
                                        op1=ALU.add).then_inc(y_added, 1)

        def diff(i, kinds):
            for k in kinds:
                dve.wait_ge(ld[k], i * (16 * LOADS[k]) + 16 * LOADS[k])
                if not (isinstance(i, int) and i == 0):
                    dve.wait_ge(w_ready[k], i)
                v_.tensor_tensor(w_f[k], staged[k][0], staged[k][1], ALU.subtract).then_inc(w_diff[k], 1)

        def step(i, first=False, last=False):
            if first:
                diff(i + 1, KIND[:2])
                diff(i, KIND[2:])
            hidden(i, 0, first)
            if not (first or last):
                diff(i + 1, KIND[:2])
            if not first:
                add(i - 1, range(0, 4))
            hidden(i, 1, first)
            if not first:
                add(i - 1, range(4, 8))
            if not last:
                diff(i + 1, KIND[2:])

        step(0, first=True)
        dve.wait_ge(dsc_in, 16)
        step(1)
        with dve.Fori(1, IT // 2 - 1) as p:
            step(p * 2)
            step(p * 2 + 1)
        step(IT - 2)
        hidden(IT - 1, 0)

        def times_s(n):
            m, c = UNIT[n]
            cs = slice(c * CH, (c + 1) * CH)
            dve.wait_ge(silu_ready, n + 1)
            v_.tensor_tensor(yT[:, m, cs], yT[:, m, cs], sT[:, m, cs], ALU.mult).then_inc(prod_ready, 1)

        def last_add(n):
            i, u = LAST[n]
            m, c = UNIT[u]
            dst = yT[:, m, c * CH:(c + 1) * CH]
            dve.wait_ge(y_ready, (IT - 2) * UNITS + n + 1)
            before = (IT - 3) * UNITS + u if i == IT - 2 else (IT - 2) * UNITS + LAST.index((IT - 2, u))
            dve.wait_ge(y_added, before + 1)
            v_.scalar_tensor_tensor(out=dst, in0=y_ps[u % 4][:, :], scalar=dsc[:, i, m:m + 1], in1=dst,
                                    op0=ALU.mult, op1=ALU.add).then_inc(y_added, 1)

        for n in range(4):
            last_add(n)
        hidden(IT - 1, 1)
        for n in range(4, 16):
            last_add(n)
            if 9 <= n < 13:
                times_s(n - 9)
        for n in range(4, UNITS):
            times_s(n)
        dve.wait_ge(xt_in, 16)
        for n, (m, c) in enumerate(UNIT[POOL_UNITS:], POOL_UNITS):
            cs = slice(c * CH, (c + 1) * CH)
            dve.wait_ge(prod_ready, n + 1)
            v_.tensor_tensor(xt[:, m, cs], xt[:, m, cs], yT[:, m, cs], ALU.add).then_inc(fin_by_dve, 1)

    @block.tensor
    def _(pe):
        mm = nc.tensor.matmul

        def gate_up(i, c, b, first=False):
            cs = slice(c * CH, (c + 1) * CH)
            for k, ps, ready, free in (("gate", gate_ps, gate_ready, sg_ready), ("up", up_ps, up_ready, hid_ready)):
                pe.wait_ge(w_ready[k], i + 1)
                if not first:
                    pe.wait_ge(free, i * NC + (c - 1))
                n = 0
                for kt in range(KT):
                    ws = slice(kt * P, (kt + 1) * P)
                    for a, x_ in ((w_h, xh), (w_h, xl), (w_l, xh)):
                        ins = mm(ps[c][:, :], a[k][b][:, ws], x_[:, kt, cs], start=(n == 0), stop=(n == 3 * KT - 1))
                        n += 1
                ins.then_inc(ready, 1)

        def y_units(i, b, units, first=False, place=None):
            pe.wait_ge(w_ready["down"], i + 1)
            for u in units:
                m, c = UNIT[u]
                ms_, cs = slice(m * P, (m + 1) * P), slice(c * CH, (c + 1) * CH)
                pe.wait_ge(h_lo, i * NC + (1 + c))
                if place is not None:
                    pe.wait_ge(y_added, (IT - 2) * UNITS + place + (u - units[0]) - 3)
                elif not (first and u < 4):
                    pe.wait_ge(y_added, i * UNITS + (u - 3))
                out = y_ps[u % 4][:, :]
                mm(out, w_h["down"][b][:, ms_], h_h[b][:, cs], start=True, stop=False)
                mm(out, w_h["down"][b][:, ms_], h_l[b][:, cs], start=False, stop=False)
                mm(out, w_l["down"][b][:, ms_], h_h[b][:, cs], start=False, stop=True).then_inc(y_ready, 1)

        gate_up(0, 0, 0, first=True)
        gate_up(0, 1, 0, first=True)
        gate_up(1, 0, 1)
        y_units(0, 0, range(0, 4), first=True)
        gate_up(1, 1, 1)
        y_units(0, 0, range(4, 8))
        with pe.Fori(1, IT // 2 - 1) as p:
            for b in range(2):
                i = p * 2 + b
                gate_up(i, 0, b)
                y_units(i - 1, 1 - b, range(0, 4))
                gate_up(i, 1, b)
                y_units(i - 1, 1 - b, range(4, 8))
        gate_up(IT - 2, 0, 0)
        y_units(IT - 3, 1, range(0, 4))
        gate_up(IT - 2, 1, 0)
        y_units(IT - 3, 1, range(4, 8))
        gate_up(IT - 1, 0, 1)
        y_units(IT - 2, 0, range(0, 4), place=0)
        gate_up(IT - 1, 1, 1)
        y_units(IT - 1, 1, range(0, 4), place=4)
        y_units(IT - 2, 0, range(4, 8), place=8)
        y_units(IT - 1, 1, range(4, 8), place=12)


def program(nc, x, xT, wq, wkv, wo, slopes, qkw, gate, up, down, down_sc, outT):
    with ExitStack() as keep_stack:
        keep = {
            "xh": keep_stack.enter_context(nc.sbuf_tensor("xh", [P, KT, TOK], F32R)),
            "xl": keep_stack.enter_context(nc.sbuf_tensor("xl", [P, KT, TOK], F32R)),
            "s": keep_stack.enter_context(nc.sbuf_tensor("s_acc", [P, KT * TOK], F32)),
        }
        keep["stage"] = keep_stack.enter_context(nc.sbuf_tensor("stage", [P, 6 * CH], F32))
        for n in ("w0_h", "w0_l"):
            keep[n] = keep_stack.enter_context(nc.sbuf_tensor(n, [P, 2 * CH], F32R))
        keep["dsc"] = keep_stack.enter_context(nc.sbuf_tensor("dsc", [P, IT, KT], F32))
        keep["dsc_in"] = keep_stack.enter_context(nc.semaphore("dsc_in"))
        for k in ("gate", "up", "down"):
            for n in ("ld", "diff", "scaled", "w_hi", "w_ready"):
                keep[f"{k}_{n}"] = keep_stack.enter_context(nc.semaphore(f"{k}_{n}"))
        with ExitStack() as stack:
            attention(nc, stack, keep, x, wq, wkv, wo, slopes, qkw, {"gate": gate, "up": up}, down_sc)
        with ExitStack() as stack:
            ffn(nc, stack, keep, xT, {"gate": gate, "up": up, "down": down}, outT)


def alibi_slopes():
    start = 2 ** (-2 ** (-(np.log2(HEADS) - 3)))
    return np.array([start * start ** i for i in range(HEADS)], dtype=np.float32)


def kernel(**inputs):
    import concourse.bacc as bacc
    from concourse.bass_utils import run_bass_kernel_spmd

    a = {n: np.asarray(v) for n, v in inputs.items()}
    put = np.ascontiguousarray
    x = a["L0_attn_x"].reshape(TOK, DM)
    arrays = {
        "x": put(x.reshape(QT, P, DM)),
        "xT": put(x.T.reshape(KT, P, TOK).transpose(1, 0, 2)),
        "wq": put(a["L0_attn_Wq"].reshape(HEADS, HD, KT, P).transpose(0, 3, 2, 1)),
        "wkv": put(np.concatenate([a[n].reshape(GROUPS, HD, KT, P).transpose(0, 3, 2, 1)
                                   for n in ("L0_attn_Wk", "L0_attn_Wv")], axis=3)),
        "wo": put(a["L0_attn_Wo"].reshape(DM, HEADS, HD).transpose(1, 2, 0)),
        "slopes": put(np.broadcast_to(alibi_slopes(), (P, HEADS))),
        "qkw": put(np.stack([a["L0_attn_q_norm_w"], a["L0_attn_k_norm_w"]], axis=1)),
        "gate_w": put(a["L0_ffn_gate_w"].reshape(KT, P, IT, P).transpose(2, 1, 0, 3)).reshape(IT, P, CH),
        "gate_z": put(a["L0_ffn_gate_z"].reshape(KT, IT, P).transpose(1, 0, 2)).reshape(IT, 1, CH),
        "gate_s": put(a["L0_ffn_gate_s"].reshape(KT, IT, P).transpose(1, 0, 2)).reshape(IT, 1, CH),
        "up_w": put(a["L0_ffn_up_w"].reshape(KT, P, IT, P).transpose(2, 1, 0, 3)).reshape(IT, P, CH),
        "up_z": put(a["L0_ffn_up_z"].reshape(KT, IT, P).transpose(1, 0, 2)).reshape(IT, 1, CH),
        "up_s": put(a["L0_ffn_up_s"].reshape(KT, IT, P).transpose(1, 0, 2)).reshape(IT, 1, CH),
        "down_w": put(a["L0_ffn_down_w"].reshape(IT, P, DM)),
        "down_z": put(a["L0_ffn_down_z"].reshape(IT, 1, DM)),
        "down_s": put(a["L0_ffn_down_s"].reshape(IT, KT, P).transpose(2, 0, 1)),
    }
    nc = bacc.Bacc("TRN2", target_bir_lowering=False, num_devices=1, dynamic_dma_scratch_size=1024)
    d = {n: nc.dram_tensor(f"in_{n}", v.shape, mybir.dt.from_np(v.dtype), kind="ExternalInput").ap()
         for n, v in arrays.items()}
    outT = nc.dram_tensor("outT", (P, KT, TOK), F32, kind="ExternalOutput").ap()
    program(nc, d["x"], d["xT"], d["wq"], d["wkv"], d["wo"], d["slopes"], d["qkw"],
            (d["gate_w"], d["gate_z"], d["gate_s"]), (d["up_w"], d["up_z"], d["up_s"]),
            (d["down_w"], d["down_z"]), d["down_s"], outT)
    r = run_bass_kernel_spmd(nc, [{f"in_{n}": v for n, v in arrays.items()}], core_ids=[0])
    got = r.results[0]["outT"]
    return put(got.transpose(1, 0, 2).reshape(DM, TOK).T).reshape(1, TOK, DM)
```
